# Optimizing a Trainium2 kernel written in Bass

```python
import numpy as np
import jax
import jax.numpy as jnp

def _softmax(x, axis=-1):
    return jax.nn.softmax(x, axis=axis)

def _gelu(x):
    return jax.nn.gelu(x, approximate=True)

def _silu(x):
    return jax.nn.silu(x)

def _sigmoid(x):
    return jax.nn.sigmoid(x)

def _layernorm(x, axis=-1, eps=1e-05):
    m = jnp.mean(x, axis=axis, keepdims=True)
    v = jnp.var(x, axis=axis, keepdims=True)
    return (x - m) / jnp.sqrt(v + eps)

def _scatter_add(tgt, idx, src, axis=0):
    return tgt.at[idx].add(src)

def _segment_sum(src, seg, n):
    return jax.ops.segment_sum(src, seg, n)
kernel_name = 'mk_xattn_seq_d2_seqx_r4_c75637'

def setup_inputs(seed: int=0):
    np.random.seed(seed)
    _w = jnp.asarray

    def _rec_inputs():
        import jax
        import jax.numpy as jnp
        _rk = jax.random.key(seed)
        x = 7.22e-05 + 1 * jax.random.normal(jax.random.fold_in(_rk, 1), (32, 128, 512), jnp.float32)
        _lenS = 128 - jax.random.randint(jax.random.fold_in(_rk, 7), (32,), 0, max(1, 128 // 4) + 1, jnp.int32)
        _lenS2 = 128 - jax.random.randint(jax.random.fold_in(_rk, 8), (32,), 0, max(1, 128 // 4) + 1, jnp.int32)
        _ctx_2048P = jax.random.normal(jax.random.fold_in(_rk, 11), (32, 16, 512), jnp.float32)
        _ctx_2048c = jax.random.dirichlet(jax.random.fold_in(_rk, 511), 0.3 * jnp.ones((16,), jnp.float32), (32, 128))
        _ctx_2048t = jnp.einsum('bsk,bkd->bsd', _ctx_2048c, _ctx_2048P)
        _ctx_2048t = _ctx_2048t * jax.lax.rsqrt(jnp.mean(jnp.square(_ctx_2048t)) + 1e-12) * 0.953939
        ctx_2048 = 4.13588e-05 + 0.999923 * (_ctx_2048t + 0.3 * jax.random.normal(jax.random.fold_in(_rk, 611), (32, 128, 512), jnp.float32))
        _validS = jnp.arange(128)[None, :] < _lenS[:, None]
        _validS2 = jnp.arange(128)[None, :] < _lenS2[:, None]
        _causal = jnp.tril(jnp.ones((128, 128), dtype=bool))
        mask_Bx1xSxS2_ff0 = jnp.where(jnp.ones((32, 1, 128, 128), dtype=bool), 0.0, -1000000000.0).astype(jnp.float32)
        return (x, ctx_2048, mask_Bx1xSxS2_ff0)
    x, ctx_2048, mask_Bx1xSxS2_ff0 = _rec_inputs()

    def _L0_xattn_setup():
        import jax, jax.numpy as jnp
        import numpy as np
        H = 512
        NH = 32
        KVH = 8
        HD = H // NH
        GROUPS = NH // KVH
        EPS = 1e-06
        B, L, S = (4, 256, 256)

        def _gqa_forward(hidden_state, encoder_hidden_state, encoder_attention_mask, Wq, bq, Wk, bk, Wv, bv, Wo, bo, gamma, beta):
            b, l, _ = hidden_state.shape
            s = encoder_hidden_state.shape[1]
            q = hidden_state @ Wq + bq
            k = encoder_hidden_state @ Wk + bk
            v = encoder_hidden_state @ Wv + bv
            q = q.reshape(b, l, KVH, GROUPS, HD).transpose(0, 2, 3, 1, 4)
            k = k.reshape(b, s, KVH, HD).transpose(0, 2, 1, 3)
            v = v.reshape(b, s, KVH, HD).transpose(0, 2, 1, 3)
            scale = 1.0 / jnp.sqrt(jnp.asarray(HD, q.dtype))
            scores = jnp.einsum('bkgld,bksd->bkgls', q, k) * scale
            scores = scores + encoder_attention_mask[:, :, None, :, :]
            attn = jax.nn.softmax(scores, axis=-1)
            out = jnp.einsum('bkgls,bksd->bkgld', attn, v)
            out = out.transpose(0, 3, 1, 2, 4).reshape(b, l, H)
            out = out @ Wo + bo
            x = out + hidden_state
            mu = jnp.mean(x, axis=-1, keepdims=True)
            var = jnp.var(x, axis=-1, keepdims=True)
            return (x - mu) * jax.lax.rsqrt(var + EPS) * gamma + beta
        key = jax.random.key(seed)
        ks = jax.random.split(key, 12)
        sd = 0.02
        return {'hidden_state': jax.random.normal(ks[0], (B, L, H), jnp.float32), 'encoder_hidden_state': jax.random.normal(ks[1], (B, S, H), jnp.float32), 'encoder_attention_mask': jnp.zeros((B, 1, L, S), jnp.float32), 'Wq': jax.random.normal(ks[2], (H, H), jnp.float32) * sd, 'bq': jnp.zeros((H,), jnp.float32), 'Wk': jax.random.normal(ks[3], (H, KVH * HD), jnp.float32) * sd, 'bk': jnp.zeros((KVH * HD,), jnp.float32), 'Wv': jax.random.normal(ks[4], (H, KVH * HD), jnp.float32) * sd, 'bv': jnp.zeros((KVH * HD,), jnp.float32), 'Wo': jax.random.normal(ks[5], (H, H), jnp.float32) * sd, 'bo': jnp.zeros((H,), jnp.float32), 'gamma': jnp.ones((H,), jnp.float32), 'beta': jnp.zeros((H,), jnp.float32)}
    _L0_xattn_all = _L0_xattn_setup()
    _L0_xattn_in = {k: v for k, v in _L0_xattn_all.items() if k in ('Wq', 'bq', 'Wk', 'bk', 'Wv', 'bv', 'Wo', 'bo', 'gamma', 'beta')}
    del _L0_xattn_all

    def _L1_xattn_setup():
        import jax, jax.numpy as jnp
        import numpy as np
        B, L, E, H = (4, 128, 512, 32)
        S = E // H
        EXTRA_MAA, EXTRA_DECAY = (32, 64)
        EPS = 1e-05

        def _ln(x, w, b):
            m = jnp.mean(x, axis=-1, keepdims=True)
            v = jnp.mean((x - m) ** 2, axis=-1, keepdims=True)
            return (x - m) * jax.lax.rsqrt(v + EPS) * w + b

        def _token_shift(xn, prev_row):
            first = (prev_row - xn[:, 0])[:, None]
            rest = xn[:, :-1] - xn[:, 1:]
            return jnp.concatenate([first, rest], axis=1)
        key = jax.random.key(seed)
        ks = jax.random.split(key, 24)
        rn = lambda k, shp, s=1.0: jax.random.normal(k, shp, dtype=jnp.float32) * s
        return dict(x=rn(ks[0], (B, L, E)), state=rn(ks[1], (B, 2 + S, E), 0.1), ln1_w=jnp.ones((E,), jnp.float32), ln1_b=jnp.zeros((E,), jnp.float32), ln2_w=jnp.ones((E,), jnp.float32), ln2_b=jnp.zeros((E,), jnp.float32), maa_x=rn(ks[2], (E,), 0.02), maa_w1=rn(ks[3], (E, 5 * EXTRA_MAA), 0.02), maa_w2=rn(ks[4], (5, EXTRA_MAA, E), 0.02), maa_stack=rn(ks[5], (5, E), 0.02), time_decay=rn(ks[6], (E,), 0.5), decay_w1=rn(ks[7], (E, EXTRA_DECAY), 0.02), decay_w2=rn(ks[8], (EXTRA_DECAY, E), 0.02), faaaa=rn(ks[9], (H, S), 0.1), Wr=rn(ks[10], (E, E), 0.02), Wk=rn(ks[11], (E, E), 0.02), Wv=rn(ks[12], (E, E), 0.02), Wg=rn(ks[13], (E, E), 0.02), Wo=rn(ks[14], (E, E), 0.02), gn_w=jnp.ones((E,), jnp.float32), gn_b=jnp.zeros((E,), jnp.float32), ffn_maa_k=rn(ks[15], (E,), 0.02), ffn_maa_r=rn(ks[16], (E,), 0.02), ffn_Wk=rn(ks[17], (E, E), 0.02), ffn_Wr=rn(ks[18], (E, E), 0.02), ffn_Wv=rn(ks[19], (E, E), 0.02), i=0)
    _L1_xattn_all = _L1_xattn_setup()
    _L1_xattn_in = {k: v for k, v in _L1_xattn_all.items() if k in ('ln1_w', 'ln1_b', 'ln2_w', 'ln2_b', 'maa_x', 'maa_w1', 'maa_w2', 'maa_stack', 'time_decay', 'decay_w1', 'decay_w2', 'faaaa', 'Wr', 'Wk', 'Wv', 'Wg', 'Wo', 'gn_w', 'gn_b', 'ffn_maa_k', 'ffn_maa_r', 'ffn_Wk', 'ffn_Wr', 'ffn_Wv')}
    del _L1_xattn_all
    return {'x': x, 'ctx_2048': ctx_2048, 'mask_Bx1xSxS2_ff0': mask_Bx1xSxS2_ff0, 'L0_xattn_Wq': _L0_xattn_in['Wq'], 'L0_xattn_bq': _L0_xattn_in['bq'], 'L0_xattn_Wk': _L0_xattn_in['Wk'], 'L0_xattn_bk': _L0_xattn_in['bk'], 'L0_xattn_Wv': _L0_xattn_in['Wv'], 'L0_xattn_bv': _L0_xattn_in['bv'], 'L0_xattn_Wo': _L0_xattn_in['Wo'], 'L0_xattn_bo': _L0_xattn_in['bo'], 'L0_xattn_gamma': _L0_xattn_in['gamma'], 'L0_xattn_beta': _L0_xattn_in['beta'], 'L1_xattn_ln1_w': _L1_xattn_in['ln1_w'], 'L1_xattn_ln1_b': _L1_xattn_in['ln1_b'], 'L1_xattn_ln2_w': _L1_xattn_in['ln2_w'], 'L1_xattn_ln2_b': _L1_xattn_in['ln2_b'], 'L1_xattn_maa_x': _L1_xattn_in['maa_x'], 'L1_xattn_maa_w1': _L1_xattn_in['maa_w1'], 'L1_xattn_maa_w2': _L1_xattn_in['maa_w2'], 'L1_xattn_maa_stack': _L1_xattn_in['maa_stack'], 'L1_xattn_time_decay': _L1_xattn_in['time_decay'], 'L1_xattn_decay_w1': _L1_xattn_in['decay_w1'], 'L1_xattn_decay_w2': _L1_xattn_in['decay_w2'], 'L1_xattn_faaaa': _L1_xattn_in['faaaa'], 'L1_xattn_Wr': _L1_xattn_in['Wr'], 'L1_xattn_Wk': _L1_xattn_in['Wk'], 'L1_xattn_Wv': _L1_xattn_in['Wv'], 'L1_xattn_Wg': _L1_xattn_in['Wg'], 'L1_xattn_Wo': _L1_xattn_in['Wo'], 'L1_xattn_gn_w': _L1_xattn_in['gn_w'], 'L1_xattn_gn_b': _L1_xattn_in['gn_b'], 'L1_xattn_ffn_maa_k': _L1_xattn_in['ffn_maa_k'], 'L1_xattn_ffn_maa_r': _L1_xattn_in['ffn_maa_r'], 'L1_xattn_ffn_Wk': _L1_xattn_in['ffn_Wk'], 'L1_xattn_ffn_Wr': _L1_xattn_in['ffn_Wr'], 'L1_xattn_ffn_Wv': _L1_xattn_in['ffn_Wv']}

def reference(x, ctx_2048, mask_Bx1xSxS2_ff0, L0_xattn_Wq, L0_xattn_bq, L0_xattn_Wk, L0_xattn_bk, L0_xattn_Wv, L0_xattn_bv, L0_xattn_Wo, L0_xattn_bo, L0_xattn_gamma, L0_xattn_beta, L1_xattn_ln1_w, L1_xattn_ln1_b, L1_xattn_ln2_w, L1_xattn_ln2_b, L1_xattn_maa_x, L1_xattn_maa_w1, L1_xattn_maa_w2, L1_xattn_maa_stack, L1_xattn_time_decay, L1_xattn_decay_w1, L1_xattn_decay_w2, L1_xattn_faaaa, L1_xattn_Wr, L1_xattn_Wk, L1_xattn_Wv, L1_xattn_Wg, L1_xattn_Wo, L1_xattn_gn_w, L1_xattn_gn_b, L1_xattn_ffn_maa_k, L1_xattn_ffn_maa_r, L1_xattn_ffn_Wk, L1_xattn_ffn_Wr, L1_xattn_ffn_Wv):
    import jax
    import jax.numpy as jnp

    def _L0_xattn_ref(hidden_state, encoder_hidden_state, encoder_attention_mask, Wq, bq, Wk, bk, Wv, bv, Wo, bo, gamma, beta):
        import jax, jax.numpy as jnp
        import numpy as np
        H = 512
        NH = 32
        KVH = 8
        HD = H // NH
        GROUPS = NH // KVH
        EPS = 1e-06
        B, L, S = (4, 256, 256)

        def _gqa_forward(hidden_state, encoder_hidden_state, encoder_attention_mask, Wq, bq, Wk, bk, Wv, bv, Wo, bo, gamma, beta):
            b, l, _ = hidden_state.shape
            s = encoder_hidden_state.shape[1]
            q = hidden_state @ Wq + bq
            k = encoder_hidden_state @ Wk + bk
            v = encoder_hidden_state @ Wv + bv
            q = q.reshape(b, l, KVH, GROUPS, HD).transpose(0, 2, 3, 1, 4)
            k = k.reshape(b, s, KVH, HD).transpose(0, 2, 1, 3)
            v = v.reshape(b, s, KVH, HD).transpose(0, 2, 1, 3)
            scale = 1.0 / jnp.sqrt(jnp.asarray(HD, q.dtype))
            scores = jnp.einsum('bkgld,bksd->bkgls', q, k) * scale
            scores = scores + encoder_attention_mask[:, :, None, :, :]
            attn = jax.nn.softmax(scores, axis=-1)
            out = jnp.einsum('bkgls,bksd->bkgld', attn, v)
            out = out.transpose(0, 3, 1, 2, 4).reshape(b, l, H)
            out = out @ Wo + bo
            x = out + hidden_state
            mu = jnp.mean(x, axis=-1, keepdims=True)
            var = jnp.var(x, axis=-1, keepdims=True)
            return (x - mu) * jax.lax.rsqrt(var + EPS) * gamma + beta
        return _gqa_forward(hidden_state, encoder_hidden_state, encoder_attention_mask, Wq, bq, Wk, bk, Wv, bv, Wo, bo, gamma, beta)

    def _L1_xattn_ref(x, state, ln1_w, ln1_b, ln2_w, ln2_b, maa_x, maa_w1, maa_w2, maa_stack, time_decay, decay_w1, decay_w2, faaaa, Wr, Wk, Wv, Wg, Wo, gn_w, gn_b, ffn_maa_k, ffn_maa_r, ffn_Wk, ffn_Wr, ffn_Wv, i):
        import jax, jax.numpy as jnp
        import numpy as np
        B, L, E, H = (4, 128, 512, 32)
        S = E // H
        EXTRA_MAA, EXTRA_DECAY = (32, 64)
        EPS = 1e-05

        def _ln(x, w, b):
            m = jnp.mean(x, axis=-1, keepdims=True)
            v = jnp.mean((x - m) ** 2, axis=-1, keepdims=True)
            return (x - m) * jax.lax.rsqrt(v + EPS) * w + b

        def _token_shift(xn, prev_row):
            first = (prev_row - xn[:, 0])[:, None]
            rest = xn[:, :-1] - xn[:, 1:]
            return jnp.concatenate([first, rest], axis=1)
        b, l = (x.shape[0], x.shape[1])
        i0 = (2 + S) * i + 0
        i1 = (2 + S) * i + 1
        xn = _ln(x, ln1_w, ln1_b)
        sx = _token_shift(xn, state[:, i1])
        xxx = jnp.tanh((xn + sx * maa_x) @ maa_w1).reshape(b, l, 5, 1, EXTRA_MAA)
        xxx = jnp.matmul(xxx, maa_w2).reshape(b, l, 5, E)
        x5 = xn[:, :, None] + sx[:, :, None] * (maa_stack + xxx)
        w = jnp.exp(-jnp.exp(time_decay + jnp.tanh(x5[:, :, 1] @ decay_w1) @ decay_w2))
        w = w.reshape(b, l, H, S)
        r = (x5[:, :, 3] @ Wr.T).reshape(b, l, H, S)
        k = (x5[:, :, 0] @ Wk.T).reshape(b, l, H, S)
        v = (x5[:, :, 2] @ Wv.T).reshape(b, l, H, S)
        g = jax.nn.silu(x5[:, :, 4] @ Wg.T)
        s0 = state[:, (2 + S) * i + 2:(2 + S) * (i + 1)].reshape(b, H, S, S)
        u = faaaa[None, :, :, None]

        def step(s, rkvw):
            r_t, k_t, v_t, w_t = rkvw
            a = k_t[:, :, :, None] * v_t[:, :, None, :]
            out = jnp.einsum('bhk,bhkd->bhd', r_t, u * a + s)
            return (a + w_t[:, :, :, None] * s, out)
        xs = tuple((jnp.moveaxis(t, 1, 0) for t in (r, k, v, w)))
        _, outs = jax.lax.scan(step, s0, xs)
        att = jnp.moveaxis(outs, 0, 1).reshape(b, l, E)
        a4 = att.reshape(b, l, H, S)
        m = jnp.mean(a4, axis=-1, keepdims=True)
        var = jnp.mean((a4 - m) ** 2, axis=-1, keepdims=True)
        att = ((a4 - m) * jax.lax.rsqrt(var + EPS)).reshape(b, l, E) * gn_w + gn_b
        x = x + att * g @ Wo.T
        xn2 = _ln(x, ln2_w, ln2_b)
        sx2 = _token_shift(xn2, state[:, i0])
        xk = xn2 + sx2 * ffn_maa_k
        xr = xn2 + sx2 * ffn_maa_r
        rr = jax.nn.sigmoid(xr @ ffn_Wr.T)
        kk = jnp.square(jax.nn.relu(xk @ ffn_Wk.T))
        x = x + rr * (kk @ ffn_Wv.T)
        return x
    x = _L0_xattn_ref(x, ctx_2048, mask_Bx1xSxS2_ff0, L0_xattn_Wq, L0_xattn_bq, L0_xattn_Wk, L0_xattn_bk, L0_xattn_Wv, L0_xattn_bv, L0_xattn_Wo, L0_xattn_bo, L0_xattn_gamma, L0_xattn_beta)
    x = _L1_xattn_ref(x, ctx_2048, L1_xattn_ln1_w, L1_xattn_ln1_b, L1_xattn_ln2_w, L1_xattn_ln2_b, L1_xattn_maa_x, L1_xattn_maa_w1, L1_xattn_maa_w2, L1_xattn_maa_stack, L1_xattn_time_decay, L1_xattn_decay_w1, L1_xattn_decay_w2, L1_xattn_faaaa, L1_xattn_Wr, L1_xattn_Wk, L1_xattn_Wv, L1_xattn_Wg, L1_xattn_Wo, L1_xattn_gn_w, L1_xattn_gn_b, L1_xattn_ffn_maa_k, L1_xattn_ffn_maa_r, L1_xattn_ffn_Wk, L1_xattn_ffn_Wr, L1_xattn_ffn_Wv, 0)
    return x

_drawn_inputs = setup_inputs


def setup_inputs(seed=0):
    import zlib

    import numpy as np

    out = dict(_drawn_inputs(seed))
    spreads = {'L0_xattn_bq': (0.0, 0.8),
     'L0_xattn_bk': (0.0, 2.0),
     'L0_xattn_bv': (0.0, 0.1),
     'L0_xattn_bo': (0.0, 0.1),
     'L0_xattn_gamma': (1.0, 0.2),
     'L0_xattn_beta': (0.0, 0.1),
     'L1_xattn_ln1_w': (1.0, 0.2),
     'L1_xattn_ln1_b': (0.0, 0.287),
     'L1_xattn_ln2_w': (1.0, 0.6),
     'L1_xattn_ln2_b': (0.0, 0.8),
     'L1_xattn_gn_w': (1.0, 0.6),
     'L1_xattn_gn_b': (0.0, 0.73)}
    factors = {'L0_xattn_Wq': 7.026,
     'L0_xattn_Wk': 6.905,
     'L1_xattn_maa_x': 8.0,
     'L1_xattn_maa_w1': 3.126,
     'L1_xattn_maa_w2': 3.113,
     'L1_xattn_maa_stack': 6.834,
     'L1_xattn_decay_w1': 8.0,
     'L1_xattn_decay_w2': 8.0,
     'L1_xattn_faaaa': 3.186,
     'L1_xattn_ffn_maa_k': 8.0,
     'L1_xattn_ffn_maa_r': 21.513,
     'L1_xattn_ffn_Wr': 4.377}
    for name, (base, spread) in spreads.items():
        noise = np.random.default_rng([zlib.crc32(name.encode()), seed]).standard_normal(out[name].shape)
        drawn = base * np.exp(spread * noise) if base else spread * noise
        out[name] = jnp.asarray(drawn.astype(out[name].dtype))
    for name, factor in factors.items():
        out[name] = (out[name] * factor).astype(out[name].dtype)
    return out
```

```python
from contextlib import ExitStack

import concourse.bass as bass
from concourse import mybir

P = 128
B, L, E = 32, 128, 512
NC = E // P
NB = 2
G = B // NB
T = NB * L
KVH, NH, HD = 8, 32, 16
GRP = NH // KVH
HC = P // HD
MAA, DEC = 32, 64
EPS0, EPS = 1e-6, 1e-5
BIG = 3.4e38

F32 = mybir.dt.float32
I32 = mybir.dt.int32
ALU = mybir.AluOpType
ACT = mybir.ActivationFunctionType

COLS = {}
for _n, _w in (("bq", 4), ("bk", 1), ("ln1_w", 4), ("ln1_b", 4), ("ln2_w", 4), ("ln2_b", 4), ("maa_x", 4),
               ("maa", 20), ("td", 4), ("u", 4), ("gn_w", 4), ("gn_b", 4), ("mk", 4), ("mr", 4)):
    COLS[_n] = (sum(w for _, w in COLS.values()), _w)
NCOL = sum(w for _, w in COLS.values())

MIX = [1, 3, 0, 2, 4]
UNIT_D = [0, 4, 1, 5, 2, 6, 3, 7]
UNITS = NC * len(UNIT_D)
SLOTS = 6
SCORES = NB * 2 * NC


class Signal:

    def __init__(self, sem, per, by=1):
        self.sem, self.per, self.by = sem, per, by

    def after(self, g, n):
        return (g * self.per + n) * self.by


class Banks:

    def __init__(self, jobs):
        self.place, self.uses = {}, {}
        for key, bank in jobs:
            n = self.uses.get(bank, 0)
            self.place[key] = (bank, n)
            self.uses[bank] = n + 1

    def of(self, key):
        return self.place[key][0]

    def earlier(self, key, g):
        k, n = self.place[key]
        return g * self.uses[k] + n

    def through(self, key, g):
        return self.earlier(key, g) + 1


def due(value):
    return not isinstance(value, int) or value > 0


def ring(jobs, banks):
    return [(key, banks[n % len(banks)]) for n, key in enumerate(jobs)]


def attention_slots():
    slots = {}

    def at(s, *step):
        slots.setdefault(s, []).append(step)

    at(0, "turn_c", 0), at(0, "turn_c", 1), at(1, "key", 0), at(1, "value", 0)
    at(2, "turn_x", 0), at(2, "turn_x", 1), at(3, "query", 0), at(3, "query", 1)
    for n in range(SCORES):
        s = 4 + n
        at(s, "score", n)
        at(s + 2, "norm", n)
        at(s + 3, "turn_p", n)
        if n % 4 == 3:
            k = n // 4
            at(s + 4, "values", k)
            if k % 2:
                at(s + 4, "gather", k // 2)
                at(s + 5, "project", k // 2)
    s += 6
    for name, after in (("norm0", 0), ("affine0", 1), ("norm1", 4), ("turn_n", 5), ("shift", 6), ("low", 7)):
        at(s + after, name, 0)
        if name == "turn_n":
            at(s + after, name, 1)
    return [slots.get(s, []) for s in range(max(slots) + 1)]


A_SLOTS = attention_slots()
CA_SLOTS = max(len(A_SLOTS), UNITS + 6)

DB_STEPS = [("D", "mean", 0), ("D", "mean", 1), ("B", "mix", 0), ("D", "var", 0), ("B", "mix", 1),
            ("B", "proj", 0), ("D", "spread", 0), ("D", "spread", 1), ("D", "groupnorm", 0), ("B", "mix", 2),
            ("B", "proj", 1), ("D", "out", 0), ("D", "out", 1), ("D", "norm2", 0), ("B", "mix", 3),
            ("B", "proj", 2), ("D", "turn_m", 0), ("D", "turn_m", 1), ("D", "shift2", 0), ("B", "mix", 4),
            ("B", "proj", 3), ("D", "ffn_k", 0), ("D", "ffn_k", 1), ("D", "ffn_r", 0), ("D", "ffn_r", 1),
            ("D", "ffn_v", 0), ("D", "ffn_v", 1), ("B", "keep", 0), ("B", "proj", 4)]


NO_PRODUCT = ("norm", "values", "gather", "norm0", "affine0", "norm1", "shift")


def x_jobs():
    a = [(s[0], s[1]) for slot in A_SLOTS for s in slot if s[0] not in NO_PRODUCT]
    b = []
    for sec, name, n in DB_STEPS:
        if sec == "B" and name == "mix":
            b += [("mix", 2 * n), ("mix", 2 * n + 1)]
        if sec == "B" and name == "proj":
            b += [("tdecay", 0)] if n == 0 else []
            b += [("proj", 2 * n), ("proj", 2 * n + 1)]
    return ring(a + b, [0, 1, 2, 4])


def y_jobs():
    c = [(("state_v", u), 5 + u % 2) for u in range(UNITS)] + [(("readout", h), 7) for h in range(NC)]
    d = [(name, n) for sec, name, n in DB_STEPS if sec == "D" and name not in ("groupnorm", "norm2", "shift2")]
    return c + ring(d, [5, 6, 7])


def build(nc, x, ctx, mask, w, out):
    XB, YB = Banks(x_jobs()), Banks(y_jobs())
    ctxs = ExitStack()
    with ctxs:
        def sb(name, shape):
            return ctxs.enter_context(nc.sbuf_tensor(name, [P] + list(shape), F32))

        def sem(name):
            return ctxs.enter_context(nc.semaphore(name))

        wq, wk, wv, wo = sb("wq", [NC, E]), sb("wk", [NC, P]), sb("wv", [NC, P]), sb("wo", [NC, E])
        w1, w2s, dw1 = sb("w1", [NC, 5 * MAA]), sb("w2s", [E]), sb("dw1", [NC, DEC])
        low2 = sb("low2", [E])
        big = {n: sb(n, [NC, E]) for n in ("wr", "wkk", "wvv", "wg", "wo2", "fk", "fr", "fv")}
        rows = sb("rows", [3 * E + P])
        bo_r, gam_r, bet_r, bv_r = (rows[:, 0:E], rows[:, E:2 * E], rows[:, 2 * E:3 * E], rows[:, 3 * E:])
        cols = sb("cols", [NCOL])
        consts = sb("consts", [P + P + P + 2 + 56])
        ident, meanb, headb = consts[:, 0:P], consts[:, P:2 * P], consts[:, 2 * P:3 * P]
        parity, ebase = consts[:, 3 * P:3 * P + 2], consts[:, 3 * P + 2:3 * P + 58]
        sel = sb("sel", [HD, P])
        ublk = sb("ublk", [NC, P])
        bsel = sb("bsel", [NC, P])
        mhalf = sb("mhalf", [NB])
        bqn, bkm = sb("bqn", [NC]), sb("bkm", [2])

        def col(name, c):
            o = COLS[name][0] + c
            return cols[:, o:o + 1]

        xin, keep = sb("xin", [NB, E]), sb("keep", [NB, E])
        cin, nmask, s0 = sb("cin", [NB, E]), sb("nmask", [NB, L]), sb("s0", [NC, NB, HD])
        kbd, vpad = sb("kbd", [NB, KVH, L]), sb("vpad", [NB, KVH, 32])
        prev, prev2 = sb("prev", [NC, NB, 2]), sb("prev2", [NC, NB])
        least, rsum, rinv = sb("least", [SCORES, 4]), sb("rsum", [SCORES, 4]), sb("rinv", [SCORES, 4])
        stats, aggr, rstd = sb("stats", [3, NB, 6]), sb("aggr", [3, NB, 2]), sb("rstd", [3, NB])
        th, th5 = sb("th", [4, T]), sb("th5", [T])
        rT, kT, vT, gT = sb("rT", [NC, T]), sb("kT", [NC, T]), sb("vT", [NC, T]), sb("gT", [NC, T])
        ws = sb("ws", [NC, 2, NB, L])
        st = sb("st", [SLOTS, 2 * T])
        rk, dg = sb("rk", [2, T]), sb("dg", [2, T])
        att = sb("att", [NC, T])
        vs = sb("vs", [T])
        U = sb("shared", [8464])
        at = [0]

        def view(n, pattern=None, **k):
            ap = U[:, at[0]:at[0] + n]
            at[0] += n
            assert at[0] <= 8464
            return ap.rearrange(pattern, **k) if pattern else ap

        xT = view(NC * T, "p (c b t) -> p c b t", c=NC, b=NB)
        cT = view(NC * T, "p (c b t) -> p c b t", c=NC, b=NB)
        qT = view(NC * T, "p (c b t) -> p c b t", c=NC, b=NB)
        pr = view(4 * 4 * L, "p (s j t) -> p s j t", s=4, j=4)
        pT = view(4 * NC * L, "p (j c t) -> p j c t", j=4, c=NC)
        oT = view(NB * NC * L, "p (b c t) -> p b c t", b=NB, c=NC)
        at[0] = 0
        xnT = view(NC * NB * (L + 1), "p (c b t) -> p c b t", c=NC, b=NB)
        sx = view(NC * T, "p (c b t) -> p c b t", c=NC, b=NB)
        x5 = view(2 * NC * T, "p (s c b t) -> p s c b t", s=2, c=NC, b=NB)
        lnb = view(NB * E, "p (b e) -> p b e", b=NB)
        dt = view(T)
        mnT = view(NC * NB * (L + 1), "p (c b t) -> p c b t", c=NC, b=NB)
        xk = view(NC * T, "p (c b t) -> p c b t", c=NC, b=NB)
        xr = view(NC * T, "p (c b t) -> p c b t", c=NC, b=NB)
        rr = xk.rearrange("p c b t -> p (c b t)").rearrange("p (b e) -> p b e", b=NB)
        e1 = lnb.rearrange("p b e -> p (b e)").rearrange("p (c b t) -> p c b t", c=NC, b=NB)
        gth = e1
        kk = mnT.rearrange("p c b t -> p (c b t)")[:, 0:NC * T].rearrange("p (c b t) -> p c b t", c=NC, b=NB)
        stf = st.ap().rearrange("p s n -> p (s n)") if hasattr(st, "ap") else st[:].rearrange("p s n -> p (s n)")
        sq = stf[:, 0:NC * T].rearrange("p (c n) -> p c n", c=NC)
        ln2 = stf[:, 0:NB * E].rearrange("p (b e) -> p b e", b=NB)
        sx2 = stf[:, NC * T:2 * NC * T].rearrange("p (c b t) -> p c b t", c=NC, b=NB)

        bank = [ctxs.enter_context(nc.psum_tensor(f"bank{n}", [P, 512], F32)) for n in range(8)]
        filled = [sem(f"bank{n}_filled") for n in range(8)]
        emptied = [sem(f"bank{n}_emptied") for n in range(8)]

        loaded_w = [sem(f"loaded_w{n}") for n in range(4)]
        loaded_x = Signal(sem("loaded_x"), 1, 16)
        loaded_c = Signal(sem("loaded_c"), 1, 16)
        loaded_m = Signal(sem("loaded_m"), 1, 16)
        loaded_s = Signal(sem("loaded_s"), 1, 16)
        stored = Signal(sem("stored"), NB, 16)
        zeroed = sem("buffers_zeroed")
        derived = sem("constants_derived")
        masked = Signal(sem("mask_negated"), 1)
        biased = Signal(sem("x_plus_bo"), NB)
        exped = Signal(sem("exp_done"), SCORES)
        inverted = Signal(sem("sums_inverted"), SCORES)
        normed = Signal(sem("probs_normed"), SCORES)
        valued = Signal(sem("values_summed"), 4)
        gathered = Signal(sem("attention_gathered"), NB)
        rows_saved = Signal(sem("prev_rows_saved"), 1)
        rows_copied = Signal(sem("prev_row_before_ln1"), 1)
        row_kept = Signal(sem("prev_row_kept"), 1)
        rows2 = Signal(sem("prev_row_before_ln2"), 1)
        st_n = [Signal(sem(f"ln{n}_stats"), NB) for n in range(3)]
        ag_n = [Signal(sem(f"ln{n}_aggr"), NB) for n in range(3)]
        rs_n = [Signal(sem(f"ln{n}_var_eps"), 1) for n in range(3)]
        pw_n = [Signal(sem(f"ln{n}_rstd"), 1) for n in range(3)]
        ap_n = [Signal(sem(f"ln{n}_applied"), NB) for n in range(3)]
        gammad = Signal(sem("gamma_done"), NB)
        betad = Signal(sem("beta_done"), NB)
        shifted = Signal(sem("shifted"), 1)
        mixed0 = Signal(sem("maa_x_mixed"), NC)
        tanhed = Signal(sem("low_tanh"), 1)
        mixed = Signal(sem("mix_done"), 10)
        decayed = Signal(sem("decay_done"), NC)
        kept = Signal(sem("x1_kept"), NB)
        gate_th = Signal(sem("gate_tanh"), 2)
        first = Signal(sem("first_state"), UNITS)
        outer = Signal(sem("outer_done"), UNITS)
        scanned = Signal(sem("scan_done"), UNITS)
        weighed = Signal(sem("state_times_r"), UNITS)
        summed = Signal(sem("state_summed"), UNITS // 2)
        rk_done = Signal(sem("r_times_k"), NC)
        diag = Signal(sem("diag_done"), NC)
        squared = Signal(sem("squared"), 2)
        newton = Signal(sem("newton"), 11)
        gn_af = Signal(sem("gn_affine"), 2)
        gated = Signal(sem("gated"), 2)
        shifted2 = Signal(sem("shifted2"), 1)
        mixk, mixr = Signal(sem("mix_k"), NC), Signal(sem("mix_r"), NC)
        relued = Signal(sem("relu_done"), 2)
        ksq = Signal(sem("relu_squared"), 2)
        rval = Signal(sem("r_times_value"), NB)
        final = Signal(sem("final_done"), NB)

        waits = {e: sem(f"waits_of_{e}") for e in ("dve", "pool")}

        def stand(eng, name):
            eng.sem_inc(waits[name], 1)

        def over(ap, n, axis):
            shape = list(ap.shape)
            return ap.unsqueeze(axis).to_broadcast(shape[:axis] + [n] + shape[axis:])

        xg = x.rearrange("(g b) l e -> g l b e", b=NB)
        cg = ctx.rearrange("(g b) l e -> g l b e", b=NB)
        mg = mask.rearrange("(g b) o l s -> g l (b o) s", b=NB)
        og = out.rearrange("(g b) l e -> g b l e", b=NB)
        sg = ctx.rearrange("(g b) l e -> g b (l e)", b=NB)

        block = ctxs.enter_context(nc.Block())

        @block.sync
        def _(sp):
            def load_c(g):
                if due(XB.through(("turn_c", 1), g - 1)):
                    sp.wait_ge(filled[XB.of(("turn_c", 1))], XB.through(("turn_c", 1), g - 1))
                sp.dma_start(cin[:], cg[g]).then_inc(loaded_c.sem, 16)

            def load_m(g):
                if due(XB.through(("score", SCORES - 1), g - 1)):
                    sp.wait_ge(emptied[XB.of(("score", SCORES - 1))], XB.through(("score", SCORES - 1), g - 1))
                sp.dma_start(nmask[:], mg[g]).then_inc(loaded_m.sem, 16)

            def load_x(g):
                if due(kept.after(g, 0)):
                    sp.wait_ge(kept.sem, kept.after(g, 0))
                if due(ap_n[1].after(g, 0)):
                    sp.wait_ge(ap_n[1].sem, ap_n[1].after(g, 0))
                sp.dma_start(xin[:], xg[g]).then_inc(loaded_x.sem, 16)

            def load_s(g):
                if due(first.after(g, 0)):
                    sp.wait_ge(first.sem, first.after(g, 0))
                src = sg[g][:, 2 * E:2 * E + HD * E].rearrange("b (c p d) -> p c b d", c=NC, p=P)
                for c in range(NC):
                    sp.dma_start(s0[:, c], src[:, c]).then_inc(loaded_s.sem, 16)

            def store(g):
                for b in range(NB):
                    sp.wait_ge(final.sem, final.after(g, b + 1))
                    sp.dma_start(og[g][b], keep[:, b]).then_inc(stored.sem, 16)

            def wload(n, dst, src):
                sp.dma_start(dst, src).then_inc(loaded_w[n], 16)

            load_c(0)
            wload(0, consts[:], w["consts"])
            wload(0, cols[:], w["columns"])
            wload(0, rows[:], w["rows"].to_broadcast([P, 3 * E + P]))
            sp.dma_start(xin[:], xg[0]).then_inc(loaded_x.sem, 16)
            for dst, n in ((wk, "wk"), (wv, "wv"), (wq, "wq"), (wo, "wo")):
                wload(1, dst[:], w[n].rearrange("(c p) n -> p c n", p=P))
            sp.dma_start(nmask[:], mg[0]).then_inc(loaded_m.sem, 16)
            wload(2, w1[:], w["w1"].rearrange("(c p) n -> p c n", p=P))
            wload(2, w2s[:], w["w2"][0:P, :])
            wload(2, low2[2 * MAA:3 * MAA, :], w["w2"][P:P + MAA, :])
            wload(2, low2[0:DEC, :], w["dw2"])
            wload(2, dw1[:], w["dw1"].rearrange("(c p) n -> p c n", p=P))
            for n in ("wr", "wkk", "wvv", "wg"):
                wload(2, big[n][:], w[n].rearrange("(c p) n -> p c n", p=P))
            load_s(0)
            wload(3, sel[:], w["sel"])
            wload(3, bsel[:], w["bsel"])
            for n in ("wo2", "fk", "fr", "fv"):
                wload(3, big[n][:], w[n].rearrange("(c p) n -> p c n", p=P))
            load_c(1)
            load_m(1)
            load_x(1)

            def turn(i):
                load_c(i + 2)
                load_m(i + 2)
                load_s(i + 1)
                store(i)
                load_x(i + 2)

            turn(0)
            with sp.Fori(1, G - 2) as i:
                turn(i)
            load_s(G - 1)
            store(G - 2)
            store(G - 1)
            if due(stored.after(G, 0)):
                sp.wait_ge(stored.sem, stored.after(G, 0))

        W_COUNT = [3 * 16, 4 * 16, 9 * 16, 6 * 16]

        def sections(eng, ca, db):
            ca(None, 0)
            db(None, 0)
            ca(0, 1)
            db(0, 1)
            with eng.Fori(1, G - 1) as i:
                ca(i, i + 1)
                db(i, i + 1)
            ca(G - 1, None)
            db(G - 1, None)

        @block.tensor
        def _(pe):
            mm, tr = nc.tensor.matmul, nc.tensor.transpose

            def turn_x(g, b):
                if b == 0:
                    pe.wait_ge(loaded_x.sem, loaded_x.after(g, 1))
                bi = XB.of(("turn_x", b))
                ps = bank[bi]
                if due(XB.earlier(("turn_x", b), g)):
                    pe.wait_ge(emptied[bi], XB.earlier(("turn_x", b), g))
                for c in range(NC):
                    last = tr(ps[:, c * P:(c + 1) * P], xin[:, b, c * P:(c + 1) * P], ident)
                last.then_inc(filled[bi], 1)

            def turn_c(g, b):
                if b == 0:
                    pe.wait_ge(loaded_c.sem, loaded_c.after(g, 1))
                bi = XB.of(("turn_c", b))
                ps = bank[bi]
                if due(XB.earlier(("turn_c", b), g)):
                    pe.wait_ge(emptied[bi], XB.earlier(("turn_c", b), g))
                for c in range(NC):
                    last = tr(ps[:, c * P:(c + 1) * P], cin[:, b, c * P:(c + 1) * P], ident)
                last.then_inc(filled[bi], 1)

            def key(g, _):
                pe.wait_ge(emptied[XB.of(("turn_c", 1))], XB.through(("turn_c", 1), g))
                bi = XB.of(("key", 0))
                ps = bank[bi]
                if due(XB.earlier(("key", 0), g)):
                    pe.wait_ge(emptied[bi], XB.earlier(("key", 0), g))
                for c in range(NC):
                    last = mm(ps[:, 0:T], wk[:, c, :], cT[:, c], start=c == 0, stop=c == NC - 1)
                last.then_inc(filled[bi], 1)

            def value(g, _):
                bi = XB.of(("value", 0))
                ps = bank[bi]
                if due(XB.earlier(("value", 0), g)):
                    pe.wait_ge(emptied[bi], XB.earlier(("value", 0), g))
                for b in range(NB):
                    for c in range(NC):
                        last = mm(ps[:, b * P:(b + 1) * P], cT[:, c, b, :], wv[:, c, :],
                                  start=c == 0, stop=c == NC - 1)
                last.then_inc(filled[bi], 1)

            def query(g, p):
                if p == 0:
                    pe.wait_ge(emptied[XB.of(("turn_x", 1))], XB.through(("turn_x", 1), g))
                bi = XB.of(("query", p))
                ps = bank[bi]
                if due(XB.earlier(("query", p), g)):
                    pe.wait_ge(emptied[bi], XB.earlier(("query", p), g))
                for q in range(2):
                    c = 2 * p + q
                    for e in range(NC):
                        last = mm(ps[:, q * T:(q + 1) * T], wq[:, e, c * P:(c + 1) * P], xT[:, e],
                                  start=e == 0, stop=e == NC - 1)
                last.then_inc(filled[bi], 1)

            def score(g, n):
                b, half, c = n // 8, n // 4 % 2, n % 4
                if n == 0:
                    pe.wait_ge(emptied[XB.of(("key", 0))], XB.through(("key", 0), g))
                if n in (0, 2):
                    pe.wait_ge(emptied[XB.of(("query", n // 2))], XB.through(("query", n // 2), g))
                bi = XB.of(("score", n))
                ps = bank[bi]
                if due(XB.earlier(("score", n), g)):
                    pe.wait_ge(emptied[bi], XB.earlier(("score", n), g))
                mm(ps[:], qT[:, c, b, :], kbd[:, b, 4 * half:4 * half + 4, :],
                   start=True, stop=True).then_inc(filled[bi], 1)

            def turn_p(g, n):
                pe.wait_ge(normed.sem, normed.after(g, n + 1))
                bi = XB.of(("turn_p", n))
                ps = bank[bi]
                if due(XB.earlier(("turn_p", n), g)):
                    pe.wait_ge(emptied[bi], XB.earlier(("turn_p", n), g))
                for j in range(4):
                    last = tr(ps[:, j * P:(j + 1) * P], pr[:, n % 4, j, :], ident)
                last.then_inc(filled[bi], 1)

            def values(g, k):
                b, half = k // 2, k % 2
                pe.wait_ge(emptied[XB.of(("turn_p", 4 * k + 3))], XB.through(("turn_p", 4 * k + 3), g))
                if k == 0:
                    pe.wait_ge(emptied[XB.of(("value", 0))], XB.through(("value", 0), g))
                if half == 0:
                    if due(gathered.after(g, b)):
                        pe.wait_ge(gathered.sem, gathered.after(g, b))
                for j in (0, 2, 1, 3):
                    h = 4 * half + j
                    r = 32 * (h // 2)
                    last = mm(bank[3][r:r + 32, :], vpad[:, b, h, :], pT[:, j], start=h % 2 == 0, stop=h % 2 == 1)
                last.then_inc(valued.sem, 1)

            def project(g, b):
                pe.wait_ge(gathered.sem, gathered.after(g, b + 1))
                bi = XB.of(("project", b))
                ps = bank[bi]
                if due(XB.earlier(("project", b), g)):
                    pe.wait_ge(emptied[bi], XB.earlier(("project", b), g))
                for c in range(NC):
                    last = mm(ps[:], oT[:, b, c, :], wo[:, c, :], start=c == 0, stop=c == NC - 1)
                last.then_inc(filled[bi], 1)

            A = dict(turn_x=turn_x, turn_c=turn_c, key=key, value=value, query=query, score=score,
                     turn_p=turn_p, values=values, project=project)

            def spread(g, u):
                h, d = u // 8, UNIT_D[u % 8]
                if u == 0:
                    pe.wait_ge(emptied[XB.of(("proj", 7))], XB.through(("proj", 7), g))
                bi = YB.of(("state_v", u))
                ps = bank[bi]
                if due(YB.earlier(("state_v", u), g)):
                    pe.wait_ge(emptied[bi], YB.earlier(("state_v", u), g))
                for q in range(2):
                    last = mm(ps[:, q * T:(q + 1) * T], sel[:, d + 8 * q, :], vT[:, h, :], start=True, stop=True)
                last.then_inc(filled[bi], 1)

            def bonus(g, h):
                pe.wait_ge(rk_done.sem, rk_done.after(g, h + 1))
                bi = YB.of(("readout", h))
                ps = bank[bi]
                if due(YB.earlier(("readout", h), g)):
                    pe.wait_ge(emptied[bi], YB.earlier(("readout", h), g))
                mm(ps[:, T:2 * T], ublk[:, h, :], rk[:, h % 2, :], start=True, stop=True).then_inc(filled[bi], 1)

            def reduce(g, q):
                m, h = q % 4, q // 4
                if m == 0:
                    bonus(g, h)
                pe.wait_ge(weighed.sem, weighed.after(g, 2 * q + 2))
                ps = bank[7]
                for u in (2 * q, 2 * q + 1):
                    for s in range(2):
                        d = UNIT_D[u % 8] + 8 * s
                        o = 24 - 8 * (d % 4)
                        last = mm(ps[32 * (d // 4):32 * (d // 4) + 32, 0:T], ebase[:, o:o + 32],
                                  st[:, u % SLOTS, s * T:(s + 1) * T], start=m == 0, stop=m == 3)
                last.then_inc(summed.sem, 1)

            def ca(gc, ga):
                if gc is None:
                    pe.wait_ge(loaded_w[0], W_COUNT[0])
                for s in range(CA_SLOTS):
                    if gc is not None and s < UNITS:
                        spread(gc, s)
                    if gc is not None and s >= 4 and s % 2 == 0 and (s - 4) // 2 < UNITS // 2:
                        reduce(gc, (s - 4) // 2)
                    if ga is not None and s < len(A_SLOTS):
                        for name, n in A_SLOTS[s]:
                            if gc is None and name == "key":
                                pe.wait_ge(loaded_w[1], W_COUNT[1])
                            if gc is None and name == "low":
                                pe.wait_ge(loaded_w[2], W_COUNT[2])
                                pe.wait_ge(zeroed, 1)
                                pe.wait_ge(derived, 1)
                            if name in A:
                                A[name](ga, n)
                            elif name in BD:
                                BD[name](ga, n)

            def turn_n(g, p):
                pe.wait_ge(ap_n[1].sem, ap_n[1].after(g, NB))
                bi = XB.of(("turn_n", p))
                ps = bank[bi]
                if due(XB.earlier(("turn_n", p), g)):
                    pe.wait_ge(emptied[bi], XB.earlier(("turn_n", p), g))
                for q in range(2):
                    for b in range(NB):
                        c = 2 * p + q
                        o = q * T + b * P
                        last = tr(ps[:, o:o + P], lnb[:, b, c * P:(c + 1) * P], ident)
                last.then_inc(filled[bi], 1)

            def low(g, _):
                pe.wait_ge(mixed0.sem, mixed0.after(g, NC))
                bi = XB.of(("low", 0))
                ps = bank[bi]
                if due(XB.earlier(("low", 0), g)):
                    pe.wait_ge(emptied[bi], XB.earlier(("low", 0), g))
                for c in range(NC):
                    mm(ps[:, 0:T], w1[:, c, 0:P], x5[:, 0, c], start=c == 0, stop=c == NC - 1)
                for c in range(NC):
                    last = mm(ps[64:96, T:2 * T], w1[:, c, P:P + MAA], x5[:, 0, c], start=c == 0, stop=c == NC - 1)
                last.then_inc(filled[bi], 1)

            def mix(g, k):
                f = MIX[k]
                if k == 0:
                    pe.wait_ge(tanhed.sem, tanhed.after(g, 1))
                for p in range(2):
                    bi = XB.of(("mix", 2 * k + p))
                    ps = bank[bi]
                    if due(XB.earlier(("mix", 2 * k + p), g)):
                        pe.wait_ge(emptied[bi], XB.earlier(("mix", 2 * k + p), g))
                    for q in range(2):
                        c = 2 * p + q
                        if f < 4:
                            last = mm(ps[:, q * T:(q + 1) * T], w2s[:, c * P:(c + 1) * P], th[:, f, :],
                                      start=True, stop=True)
                        else:
                            last = mm(ps[:, q * T:(q + 1) * T], low2[64:96, c * P:(c + 1) * P], th5[64:96, :],
                                      start=True, stop=True)
                    last.then_inc(filled[bi], 1)

            def proj(g, k):
                pe.wait_ge(mixed.sem, mixed.after(g, 2 * k + 2))
                if k == 0:
                    bi = XB.of(("tdecay", 0))
                    ps = bank[bi]
                    if due(XB.earlier(("tdecay", 0), g)):
                        pe.wait_ge(emptied[bi], XB.earlier(("tdecay", 0), g))
                    for c in range(NC):
                        last = mm(ps[0:DEC, 0:T], dw1[:, c, :], x5[:, 0, c], start=c == 0, stop=c == NC - 1)
                    last.then_inc(filled[bi], 1)
                    pe.wait_ge(emptied[XB.of(("tdecay", 0))], XB.through(("tdecay", 0), g))
                    for p in range(2):
                        bi = XB.of(("proj", p))
                        ps = bank[bi]
                        if due(XB.earlier(("proj", p), g)):
                            pe.wait_ge(emptied[bi], XB.earlier(("proj", p), g))
                        for q in range(2):
                            c = 2 * p + q
                            last = mm(ps[:, q * T:(q + 1) * T], low2[0:DEC, c * P:(c + 1) * P], dt[0:DEC, :],
                                      start=True, stop=True)
                        last.then_inc(filled[bi], 1)
                    return
                wt = big[("wr", "wkk", "wvv", "wg")[k - 1]]
                for p in range(2):
                    bi = XB.of(("proj", 2 * k + p))
                    ps = bank[bi]
                    if due(XB.earlier(("proj", 2 * k + p), g)):
                        pe.wait_ge(emptied[bi], XB.earlier(("proj", 2 * k + p), g))
                    for q in range(2):
                        c = 2 * p + q
                        for e in range(NC):
                            last = mm(ps[:, q * T:(q + 1) * T], wt[:, e, c * P:(c + 1) * P], x5[:, k % 2, e],
                                      start=e == 0, stop=e == NC - 1)
                    last.then_inc(filled[bi], 1)

            def mean(g, p):
                pe.wait_ge(emptied[YB.of(("readout", 2 * p + 1))], YB.through(("readout", 2 * p + 1), g))
                bi = YB.of(("mean", p))
                ps = bank[bi]
                if due(YB.earlier(("mean", p), g)):
                    pe.wait_ge(emptied[bi], YB.earlier(("mean", p), g))
                for q in range(2):
                    last = mm(ps[:, q * T:(q + 1) * T], meanb, att[:, 2 * p + q, :], start=True, stop=True)
                last.then_inc(filled[bi], 1)

            def var(g, _):
                pe.wait_ge(squared.sem, squared.after(g, 2))
                bi = YB.of(("var", 0))
                ps = bank[bi]
                if due(YB.earlier(("var", 0), g)):
                    pe.wait_ge(emptied[bi], YB.earlier(("var", 0), g))
                for c in range(NC):
                    last = mm(ps[32 * c:32 * c + 32, 0:T], meanb[:, 0:32], sq[:, c, :], start=True, stop=True)
                last.then_inc(filled[bi], 1)

            def spread_rstd(g, p):
                pe.wait_ge(newton.sem, newton.after(g, 11))
                bi = YB.of(("spread", p))
                ps = bank[bi]
                if due(YB.earlier(("spread", p), g)):
                    pe.wait_ge(emptied[bi], YB.earlier(("spread", p), g))
                for q in range(2):
                    last = mm(ps[:, q * T:(q + 1) * T], bsel[:, 2 * p + q, :], dg[:, 0, :], start=True, stop=True)
                last.then_inc(filled[bi], 1)

            def out_(g, b):
                pe.wait_ge(gated.sem, gated.after(g, 2))
                bi = YB.of(("out", b))
                ps = bank[bi]
                if due(YB.earlier(("out", b), g)):
                    pe.wait_ge(emptied[bi], YB.earlier(("out", b), g))
                for c in range(NC):
                    last = mm(ps[:], att[:, c, b * P:(b + 1) * P], big["wo2"][:, c, :], start=c == 0, stop=c == NC - 1)
                last.then_inc(filled[bi], 1)

            def turn_m(g, p):
                pe.wait_ge(ap_n[2].sem, ap_n[2].after(g, NB))
                bi = YB.of(("turn_m", p))
                ps = bank[bi]
                if due(YB.earlier(("turn_m", p), g)):
                    pe.wait_ge(emptied[bi], YB.earlier(("turn_m", p), g))
                for q in range(2):
                    for b in range(NB):
                        c = 2 * p + q
                        o = q * T + b * P
                        last = tr(ps[:, o:o + P], ln2[:, b, c * P:(c + 1) * P], ident)
                last.then_inc(filled[bi], 1)

            def ffn_k(g, p):
                pe.wait_ge(mixk.sem, mixk.after(g, NC))
                bi = YB.of(("ffn_k", p))
                ps = bank[bi]
                if due(YB.earlier(("ffn_k", p), g)):
                    pe.wait_ge(emptied[bi], YB.earlier(("ffn_k", p), g))
                for q in range(2):
                    c = 2 * p + q
                    for e in range(NC):
                        last = mm(ps[:, q * T:(q + 1) * T], big["fk"][:, e, c * P:(c + 1) * P], xk[:, e],
                                  start=e == 0, stop=e == NC - 1)
                last.then_inc(filled[bi], 1)

            def ffn_r(g, b):
                pe.wait_ge(mixr.sem, mixr.after(g, NC))
                bi = YB.of(("ffn_r", b))
                ps = bank[bi]
                if due(YB.earlier(("ffn_r", b), g)):
                    pe.wait_ge(emptied[bi], YB.earlier(("ffn_r", b), g))
                for c in range(NC):
                    last = mm(ps[:], xr[:, c, b, :], big["fr"][:, c, :], start=c == 0, stop=c == NC - 1)
                last.then_inc(filled[bi], 1)

            def ffn_v(g, b):
                pe.wait_ge(ksq.sem, ksq.after(g, 2))
                bi = YB.of(("ffn_v", b))
                ps = bank[bi]
                if due(YB.earlier(("ffn_v", b), g)):
                    pe.wait_ge(emptied[bi], YB.earlier(("ffn_v", b), g))
                for c in range(NC):
                    last = mm(ps[:], kk[:, c, b, :], big["fv"][:, c, :], start=c == 0, stop=c == NC - 1)
                last.then_inc(filled[bi], 1)

            BD = dict(turn_n=turn_n, low=low, mix=mix, proj=proj, mean=mean, var=var, spread=spread_rstd, out=out_, turn_m=turn_m,
                      ffn_k=ffn_k, ffn_r=ffn_r, ffn_v=ffn_v)

            def db(gd, gb):
                for sec, name, n in DB_STEPS:
                    g = gd if sec == "D" else gb
                    if g is not None and name in BD:
                        BD[name](g, n)
                if gd is None:
                    pe.wait_ge(loaded_w[3], W_COUNT[3])

            sections(pe, ca, db)

        @block.scalar
        def _(act):
            fn = nc.scalar.activation

            def evac_turn(name, dst):
                def step(g, b):
                    if b == 0 and name == "turn_c":
                        if due(XB.through(("proj", 9), g - 1)):
                            act.wait_ge(emptied[XB.of(("proj", 9))], XB.through(("proj", 9), g - 1))
                        if due(final.after(g - 1, 0)):
                            act.wait_ge(final.sem, final.after(g - 1, 0))
                    bi = XB.of((name, b))
                    ps = bank[bi]
                    act.wait_ge(filled[bi], XB.through((name, b), g))
                    fn(dst[:, :, b, :], ps[:].rearrange("p (c t) -> p c t", c=NC), ACT.Copy).then_inc(emptied[bi], 1)
                return step

            def key(g, _):
                if due(XB.through(("score", SCORES - 1), g - 1)):
                    act.wait_ge(emptied[XB.of(("score", SCORES - 1))], XB.through(("score", SCORES - 1), g - 1))
                bi = XB.of(("key", 0))
                ps = bank[bi]
                act.wait_ge(filled[bi], XB.through(("key", 0), g))
                for h in range(KVH):
                    r = slice(32 * (h // 2), 32 * (h // 2) + 32)
                    last = fn(kbd[r, :, h, :], ps[r, 0:T].rearrange("p (b t) -> p b t", b=NB), ACT.Identity,
                              bias=bkm[r, h % 2:h % 2 + 1], scale=parity[r, h % 2:h % 2 + 1])
                last.then_inc(emptied[bi], 1)

            def query(g, p):
                bi = XB.of(("query", p))
                ps = bank[bi]
                act.wait_ge(filled[bi], XB.through(("query", p), g))
                for q in range(2):
                    c = 2 * p + q
                    last = fn(qT[:, c], ps[:, q * T:(q + 1) * T].rearrange("p (b t) -> p b t", b=NB), ACT.Identity,
                              bias=bqn[:, c:c + 1], scale=-0.25)
                last.then_inc(emptied[bi], 1)

            def score(g, n):
                act.wait_ge(emptied[XB.of(("score", n))], XB.through(("score", n), g))
                for j in range(4):
                    last = fn(pr[:, n % 4, j, :], pr[:, n % 4, j, :], ACT.Exp, bias=least[:, n, j:j + 1], scale=-1.0,
                              accum_out=rsum[:, n, j:j + 1])
                last.then_inc(exped.sem, 1)

            def turn_p(g, n):
                if n % 4 == 0:
                    if due(valued.after(g, n // 4)):
                        act.wait_ge(valued.sem, valued.after(g, n // 4))
                bi = XB.of(("turn_p", n))
                ps = bank[bi]
                act.wait_ge(filled[bi], XB.through(("turn_p", n), g))
                fn(pT[:, :, n % 4, :], ps[:].rearrange("p (j t) -> p j t", j=4), ACT.Copy).then_inc(emptied[bi], 1)

            def gather(g, b):
                act.wait_ge(valued.sem, valued.after(g, 2 * b + 2))
                fn(oT[:, b], bank[3][:].rearrange("p (c t) -> p c t", c=NC), ACT.Copy).then_inc(gathered.sem, 1)

            A = dict(turn_x=evac_turn("turn_x", xT), turn_c=evac_turn("turn_c", cT), key=key, query=query,
                     score=score, turn_p=turn_p, gather=gather)

            def ca(gc, ga):
                if gc is None:
                    act.wait_ge(zeroed, 1)
                    act.wait_ge(derived, 1)
                if ga is None:
                    return
                for slot in A_SLOTS:
                    for name, n in slot:
                        if name in A:
                            A[name](ga, n)
                        elif name in BD:
                            BD[name](ga, n)

            def halves(ps, q):
                return ps[:, q * T:(q + 1) * T].rearrange("p (b t) -> p b t", b=NB)

            def turn_n(g, p):
                bi = XB.of(("turn_n", p))
                ps = bank[bi]
                act.wait_ge(filled[bi], XB.through(("turn_n", p), g))
                for q in range(2):
                    c = 2 * p + q
                    last = fn(xnT[:, c, :, 1:], halves(ps, q), ACT.Identity, bias=col("ln1_b", c),
                              scale=col("ln1_w", c))
                last.then_inc(emptied[bi], 1)

            def low(g, _):
                bi = XB.of(("low", 0))
                ps = bank[bi]
                act.wait_ge(filled[bi], XB.through(("low", 0), g))
                for f in range(4):
                    r = slice(32 * f, 32 * f + 32)
                    fn(th[r, f, :], ps[r, 0:T], ACT.Tanh)
                fn(th5[64:96, :], ps[64:96, T:2 * T], ACT.Tanh).then_inc(emptied[bi], 1)
                act.wait_ge(emptied[XB.of(("low", 0))], XB.through(("low", 0), g))
                act.sem_inc(tanhed.sem, 1)

            def keep_x1(g, _):
                if due(stored.after(g, 0)):
                    act.wait_ge(stored.sem, stored.after(g, 0))
                act.wait_ge(betad.sem, betad.after(g, NB))
                for b in range(NB):
                    fn(keep[:, b, :], xin[:, b, :], ACT.Copy).then_inc(kept.sem, 1)

            def proj(g, k):
                if k == 0:
                    bi = XB.of(("tdecay", 0))
                    ps = bank[bi]
                    act.wait_ge(filled[bi], XB.through(("tdecay", 0), g))
                    fn(dt[0:DEC, :], ps[0:DEC, 0:T], ACT.Tanh).then_inc(emptied[bi], 1)
                    if due(YB.through(("readout", NC - 1), g - 1)):
                        act.wait_ge(emptied[YB.of(("readout", NC - 1))], YB.through(("readout", NC - 1), g - 1))
                for p in range(2):
                    bi = XB.of(("proj", 2 * k + p))
                    ps = bank[bi]
                    act.wait_ge(filled[bi], XB.through(("proj", 2 * k + p), g))
                    if k == 0:
                        for q in range(2):
                            last = fn(e1[:, 2 * p + q], halves(ps, q), ACT.Exp, bias=col("td", 2 * p + q))
                        last.then_inc(emptied[bi], 1)
                        act.wait_ge(emptied[XB.of(("proj", p))], XB.through(("proj", p), g))
                        for q in range(2):
                            c = 2 * p + q
                            for s in range(2):
                                last = fn(ws[:, c, s, :, 1:], e1[:, c, :, 0:L - 1], ACT.Exp, scale=-1.0)
                            last.then_inc(decayed.sem, 1)
                    elif k < 4:
                        dst = (rT, kT, vT)[k - 1]
                        fn(dst[:, 2 * p:2 * p + 2, :], ps[:].rearrange("p (c n) -> p c n", c=2),
                           ACT.Copy).then_inc(emptied[bi], 1)
                    else:
                        fn(gth[:, 2 * p:2 * p + 2].rearrange("p c b t -> p (c b t)"), ps[:], ACT.Tanh,
                           scale=0.5).then_inc(gate_th.sem, 1)

            def var(g, _):
                for p in range(2):
                    act.wait_ge(emptied[YB.of(("mean", p))], YB.through(("mean", p), g))
                    fn(sq[:, 2 * p:2 * p + 2, :], att[:, 2 * p:2 * p + 2, :], ACT.Square).then_inc(squared.sem, 1)

            def turn_m(g, p):
                bi = YB.of(("turn_m", p))
                ps = bank[bi]
                act.wait_ge(filled[bi], YB.through(("turn_m", p), g))
                for q in range(2):
                    c = 2 * p + q
                    last = fn(mnT[:, c, :, 1:], halves(ps, q), ACT.Identity, bias=col("ln2_b", c),
                              scale=col("ln2_w", c))
                last.then_inc(emptied[bi], 1)

            def ffn_k(g, p):
                bi = YB.of(("ffn_k", p))
                ps = bank[bi]
                act.wait_ge(filled[bi], YB.through(("ffn_k", p), g))
                act.wait_ge(mixr.sem, mixr.after(g, NC))
                v = kk[:, 2 * p:2 * p + 2].rearrange("p c b t -> p (c b t)")
                fn(v, ps[:], ACT.Relu).then_inc(emptied[bi], 1)
                act.wait_ge(emptied[YB.of(("ffn_k", p))], YB.through(("ffn_k", p), g))
                fn(v, v, ACT.Square).then_inc(ksq.sem, 1)

            def ffn_r(g, b):
                bi = YB.of(("ffn_r", b))
                ps = bank[bi]
                act.wait_ge(filled[bi], YB.through(("ffn_r", b), g))
                fn(rr[:, b, :], ps[:], ACT.Tanh, scale=0.5).then_inc(emptied[bi], 1)

            BD = dict(turn_n=turn_n, low=low, keep=keep_x1, proj=proj, var=var, turn_m=turn_m, ffn_k=ffn_k,
                      ffn_r=ffn_r)

            def db(gd, gb):
                for sec, name, n in DB_STEPS:
                    g = gd if sec == "D" else gb
                    if g is not None and name in BD:
                        BD[name](g, n)

            sections(act, ca, db)

        @block.gpsimd
        def _(pool):
            tt = nc.gpsimd.tensor_tensor

            def turn_x(g, b):
                pool.wait_ge(filled[XB.of(("turn_x", b))], XB.through(("turn_x", b), g))
                if b == 0:
                    pool.wait_ge(loaded_x.sem, loaded_x.after(g, 1))
                tt(xin[:, b, :], xin[:, b, :], bo_r, ALU.add).then_inc(biased.sem, 1)

            def negate(g):
                pool.wait_ge(loaded_m.sem, loaded_m.after(g, 1))
                stand(pool, "pool")
                nc.gpsimd.tensor_scalar(nmask[:], nmask[:], -1.0, 0.0, ALU.mult, ALU.add).then_inc(masked.sem, 1)

            def norm(g, n):
                pool.wait_ge(inverted.sem, inverted.after(g, n + 1))
                v = pr[:, n % 4]
                tt(v, v, rinv[:, n, :].unsqueeze(2).to_broadcast([P, 4, L]), ALU.mult).then_inc(normed.sem, 1)

            def first_state(g, u):
                h, d = u // 8, UNIT_D[u % 8]
                if u == 0:
                    pool.wait_ge(loaded_s.sem, loaded_s.after(g * NC, NC))
                    if due(final.after(g, 0)):
                        pool.wait_ge(final.sem, final.after(g, 0))
                if u >= SLOTS:
                    pool.wait_ge(summed.sem, summed.after(g, (u - SLOTS) // 2 + 1))
                if u == 0 or u >= SLOTS:
                    stand(pool, "pool")
                dst = st[:, u % SLOTS, :].rearrange("p (d b t) -> p d b t", d=2, b=NB)[:, :, :, 0]
                src = s0[:, h, :, d:d + 9:8].rearrange("p b d -> p d b")
                nc.gpsimd.tensor_copy(dst, src).then_inc(first.sem, 1)

            def r_times_k(g, h):
                if h == 0:
                    pool.wait_ge(emptied[XB.of(("proj", 5))], XB.through(("proj", 5), g))
                if h >= 2:
                    pool.wait_ge(filled[YB.of(("readout", h - 2))], YB.through(("readout", h - 2), g))
                tt(rk[:, h % 2, :], rT[:, h, :], kT[:, h, :], ALU.mult).then_inc(rk_done.sem, 1)

            def ca(gc, ga):
                for s in range(CA_SLOTS):
                    if gc is not None and s < UNITS:
                        first_state(gc, s)
                    if gc is not None and s < UNITS and s % 8 == 0:
                        r_times_k(gc, s // 8)
                    if ga is not None and s < len(A_SLOTS):
                        if s == 2:
                            negate(ga)
                        for name, n in A_SLOTS[s]:
                            if name == "turn_x":
                                turn_x(ga, n)
                            if name == "norm":
                                norm(ga, n)
                            elif name in BD:
                                BD[name](ga, n)

            def affine0(g, _):
                for b in range(NB):
                    pool.wait_ge(ap_n[0].sem, ap_n[0].after(g, b + 1))
                    tt(xin[:, b, :], xin[:, b, :], gam_r, ALU.mult).then_inc(gammad.sem, 1)
                for b in range(NB):
                    pool.wait_ge(gammad.sem, gammad.after(g, b + 1))
                    tt(xin[:, b, :], xin[:, b, :], bet_r, ALU.add).then_inc(betad.sem, 1)

            def mix(g, k):
                for p in range(2):
                    pool.wait_ge(emptied[XB.of(("mix", 2 * k + p))], XB.through(("mix", 2 * k + p), g))
                    v = x5[:, k % 2, 2 * p:2 * p + 2]
                    tt(v, v, xnT[:, 2 * p:2 * p + 2, :, 1:], ALU.add).then_inc(mixed.sem, 1)

            def inverse_root(n):
                def step(g, _):
                    pool.wait_ge(rs_n[n].sem, rs_n[n].after(g, 1))
                    v = rstd[:, n, :]
                    tt(v, v, mhalf[:], ALU.pow).then_inc(pw_n[n].sem, 1)
                return step

            BD = dict(norm0=inverse_root(0), norm1=inverse_root(1), norm2=inverse_root(2), affine0=affine0, mix=mix)

            def db(gd, gb):
                for sec, name, n in DB_STEPS:
                    g = gd if sec == "D" else gb
                    if g is not None and name in BD:
                        BD[name](g, n)

            nc.gpsimd.memset(kbd[:], 0.0)
            nc.gpsimd.memset(vpad[:], 0.0)
            nc.gpsimd.memset(th[:], 0.0)
            nc.gpsimd.memset(mhalf[:], -0.5)
            nc.gpsimd.memset(ws[:], 0.0).then_inc(zeroed, 1)
            pool.wait_ge(zeroed, 1)
            pool.wait_ge(loaded_w[0], W_COUNT[0])
            sections(pool, ca, db)

        @block.vector
        def _(dve):
            tt, ts, stt = nc.vector.tensor_tensor, nc.vector.tensor_scalar, nc.vector.scalar_tensor_tensor

            def key(g, _):
                dve.wait_ge(emptied[XB.of(("turn_c", 1))], XB.through(("turn_c", 1), g))
                nc.vector.tensor_copy(prev[:], cT[:, :, :, 0:2]).then_inc(rows_saved.sem, 1)

            def value(g, _):
                if due(valued.after(g, 0)):
                    dve.wait_ge(valued.sem, valued.after(g, 0))
                bi = XB.of(("value", 0))
                ps = bank[bi]
                dve.wait_ge(filled[bi], XB.through(("value", 0), g))
                pv = ps[:, 0:T].rearrange("p (b h q d) -> p b h q d", b=NB, q=2, d=HD)
                vp = vpad[:].rearrange("p b (h q) n -> p b h q n", q=2)
                bv = bv_r.rearrange("p (h q d) -> p h q d", q=2, d=HD)
                for q in range(2):
                    last = tt(vp[:, :, :, q, q * HD:(q + 1) * HD], pv[:, :, :, q, :], over(bv[:, :, q, :], NB, 1),
                              ALU.add)
                last.then_inc(emptied[bi], 1)

            def score(g, n):
                if n == 0:
                    dve.wait_ge(masked.sem, masked.after(g, 1))
                    if due(XB.through(("proj", 9), g - 1)):
                        dve.wait_ge(emptied[XB.of(("proj", 9))], XB.through(("proj", 9), g - 1))
                    if due(final.after(g - 1, 0)):
                        dve.wait_ge(final.sem, final.after(g - 1, 0))
                if n >= 4 and XB.of(("turn_p", n - 4)) != XB.of(("score", n)):
                    dve.wait_ge(filled[XB.of(("turn_p", n - 4))], XB.through(("turn_p", n - 4), g))
                bi = XB.of(("score", n))
                ps = bank[bi]
                dve.wait_ge(filled[bi], XB.through(("score", n), g))
                stand(dve, "dve")
                for j in range(4):
                    last = nc.vector.tensor_tensor_reduce(pr[:, n % 4, j, :], ps[:, j * P:(j + 1) * P],
                                                          nmask[:, n // 8, :], 1.0, BIG, ALU.add, ALU.min,
                                                          least[:, n, j:j + 1])
                last.then_inc(emptied[bi], 1)

            def norm(g, n):
                dve.wait_ge(exped.sem, exped.after(g, n + 1))
                nc.vector.reciprocal(rinv[:, n, :], rsum[:, n, :]).then_inc(inverted.sem, 1)

            def project(g, b):
                dve.wait_ge(biased.sem, biased.after(g, b + 1))
                bi = XB.of(("project", b))
                ps = bank[bi]
                dve.wait_ge(filled[bi], XB.through(("project", b), g))
                tt(xin[:, b, :], ps[:], xin[:, b, :], ALU.add).then_inc(emptied[bi], 1)

            A = dict(key=key, value=value, score=score, norm=norm, project=project)

            def outer_(g, u):
                h = u // 8
                if u == 0:
                    dve.wait_ge(emptied[XB.of(("proj", 5))], XB.through(("proj", 5), g))
                    if due(final.after(g, 0)):
                        dve.wait_ge(final.sem, final.after(g, 0))
                if u >= SLOTS:
                    dve.wait_ge(summed.sem, summed.after(g, (u - SLOTS) // 2 + 1))
                bi = YB.of(("state_v", u))
                ps = bank[bi]
                dve.wait_ge(filled[bi], YB.through(("state_v", u), g))
                dst = st[:, u % SLOTS, :].rearrange("p (d b t) -> p d b t", d=2, b=NB)[:, :, :, 1:]
                src = ps[:].rearrange("p (d b t) -> p d b t", d=2, b=NB)[:, :, :, 0:L - 1]
                kv = kT[:, h, :].rearrange("p (b t) -> p b t", b=NB)[:, :, 0:L - 1]
                tt(dst, src, over(kv, 2, 1), ALU.mult).then_inc(emptied[bi], 1)

            def scan(g, u):
                h = u // 8
                if u % 16 == 0:
                    dve.wait_ge(decayed.sem, decayed.after(g, 2 * (u // 16) + 2))
                dve.wait_ge(emptied[YB.of(("state_v", u))], YB.through(("state_v", u), g))
                dve.wait_ge(first.sem, first.after(g, u + 1))
                v = st[:, u % SLOTS, :]
                nc.vector.tensor_tensor_scan(v, ws[:, h].rearrange("p d b t -> p (d b t)"), v, 0.0,
                                             ALU.mult, ALU.add).then_inc(scanned.sem, 1)

            def weigh(g, u):
                dve.wait_ge(scanned.sem, scanned.after(g, u + 1))
                v = st[:, u % SLOTS, :].rearrange("p (d n) -> p d n", d=2)
                tt(v, v, over(rT[:, u // 8, :], 2, 1), ALU.mult).then_inc(weighed.sem, 1)

            def readout(g, h):
                bi = YB.of(("readout", h))
                ps = bank[bi]
                dve.wait_ge(filled[bi], YB.through(("readout", h), g))
                dve.wait_ge(summed.sem, summed.after(g, 4 * h + 4))
                tt(dg[:, h % 2, :], ps[:, T:2 * T], vT[:, h, :], ALU.mult).then_inc(diag.sem, 1)
                dve.wait_ge(diag.sem, diag.after(g, h + 1))
                tt(att[:, h, :], ps[:, 0:T], dg[:, h % 2, :], ALU.add).then_inc(emptied[bi], 1)

            def ca(gc, ga):
                if ga is not None and gc is None:
                    dve.wait_ge(loaded_w[0], W_COUNT[0])
                    o = COLS["bq"][0]
                    ts(bqn[:], cols[:, o:o + NC], -0.25, None, ALU.mult)
                    ts(bkm[:], parity, col("bk", 0), None, ALU.mult)
                    for c in range(NC):
                        last = ts(ublk[:, c, :], headb, col("u", c), None, ALU.mult)
                    last.then_inc(derived, 1)
                    dve.wait_ge(zeroed, 1)
                for s in range(CA_SLOTS):
                    if gc is not None:
                        if s >= 11 and (s - 11) % 8 == 0:
                            readout(gc, (s - 11) // 8)
                        if s < UNITS:
                            outer_(gc, s)
                        if 1 <= s <= UNITS:
                            scan(gc, s - 1)
                        if 2 <= s <= UNITS + 1:
                            weigh(gc, s - 2)
                    if ga is not None and s < len(A_SLOTS):
                        for name, n in A_SLOTS[s]:
                            if name in A:
                                A[name](ga, n)
                            elif name in BD:
                                BD[name](ga, n)

            def layernorm(g, n, src, dst, eps):
                for b in range(NB):
                    nc.vector.bn_stats(stats[:, n, b, :], src[:, b, :]).then_inc(st_n[n].sem, 1)
                for b in range(NB):
                    dve.wait_ge(st_n[n].sem, st_n[n].after(g, b + 1))
                    stand(dve, "dve")
                    nc.vector.bn_aggr(aggr[:, n, b, :], stats[:, n, b, :]).then_inc(ag_n[n].sem, 1)
                dve.wait_ge(ag_n[n].sem, ag_n[n].after(g, NB))
                ts(rstd[:, n, :], aggr[:, n, :, 1], eps, None, ALU.add).then_inc(rs_n[n].sem, 1)
                dve.wait_ge(pw_n[n].sem, pw_n[n].after(g, 1))
                for b in range(NB):
                    ts(dst[:, b, :], src[:, b, :], aggr[:, n, b, 0:1], rstd[:, n, b:b + 1], ALU.subtract,
                       ALU.mult).then_inc(ap_n[n].sem, 1)

            def norm0(g, _):
                dve.wait_ge(emptied[XB.of(("project", 1))], XB.through(("project", 1), g))
                layernorm(g, 0, xin, xin, EPS0)

            def norm1(g, _):
                dve.wait_ge(betad.sem, betad.after(g, NB))
                layernorm(g, 1, xin, lnb, EPS)
                dve.wait_ge(rows_saved.sem, rows_saved.after(g, 1))
                nc.vector.tensor_copy(xnT[:, :, :, 0], prev[:, :, :, 1]).then_inc(rows_copied.sem, 1)

            def shift(g, _):
                dve.wait_ge(emptied[XB.of(("turn_n", 1))], XB.through(("turn_n", 1), g))
                dve.wait_ge(rows_copied.sem, rows_copied.after(g, 1))
                tt(sx[:], xnT[:, :, :, 0:L], xnT[:, :, :, 1:], ALU.subtract).then_inc(shifted.sem, 1)
                dve.wait_ge(shifted.sem, shifted.after(g, 1))
                for c in range(NC):
                    stt(out=x5[:, 0, c], in0=sx[:, c], scalar=col("maa_x", c), in1=xnT[:, c, :, 1:],
                        op0=ALU.mult, op1=ALU.add).then_inc(mixed0.sem, 1)

            def mix(g, k):
                f = MIX[k]
                if k == 0:
                    dve.wait_ge(filled[XB.of(("low", 0))], XB.through(("low", 0), g))
                elif k == 2:
                    dve.wait_ge(filled[XB.of(("tdecay", 0))], XB.through(("tdecay", 0), g))
                elif k >= 3:
                    dve.wait_ge(filled[XB.of(("proj", 2 * k - 3))], XB.through(("proj", 2 * k - 3), g))
                for p in range(2):
                    bi = XB.of(("mix", 2 * k + p))
                    ps = bank[bi]
                    dve.wait_ge(filled[bi], XB.through(("mix", 2 * k + p), g))
                    for q in range(2):
                        c = 2 * p + q
                        last = stt(out=x5[:, k % 2, c], in0=ps[:, q * T:(q + 1) * T].rearrange(
                            "p (b t) -> p b t", b=NB), scalar=col("maa", f * NC + c), in1=sx[:, c],
                            op0=ALU.add, op1=ALU.mult)
                    last.then_inc(emptied[bi], 1)

            def keep_row(g, _):
                dve.wait_ge(rows_saved.sem, rows_saved.after(g, 1))
                nc.vector.tensor_copy(prev2[:], prev[:, :, :, 0]).then_inc(row_kept.sem, 1)

            def proj(g, k):
                if k < 4:
                    return
                for p in range(2):
                    bi = XB.of(("proj", 2 * k + p))
                    ps = bank[bi]
                    dve.wait_ge(filled[bi], XB.through(("proj", 2 * k + p), g))
                    dve.wait_ge(gate_th.sem, gate_th.after(g, p + 1))
                    stt(out=gT[:, 2 * p:2 * p + 2, :], in0=gth[:, 2 * p:2 * p + 2].rearrange(
                        "p c b t -> p c (b t)"), scalar=1.0, in1=ps[:].rearrange("p (c n) -> p c n", c=2),
                        op0=ALU.add, op1=ALU.mult).then_inc(emptied[bi], 1)

            def mean(g, p):
                dve.wait_ge(emptied[YB.of(("readout", 2 * p + 1))], YB.through(("readout", 2 * p + 1), g))
                bi = YB.of(("mean", p))
                ps = bank[bi]
                dve.wait_ge(filled[bi], YB.through(("mean", p), g))
                v = att[:, 2 * p:2 * p + 2, :]
                tt(v, v, ps[:].rearrange("p (c n) -> p c n", c=2), ALU.subtract).then_inc(emptied[bi], 1)

            def var(g, _):
                y, h = dg[:, 0, :], dg[:, 1, :]
                bi = YB.of(("var", 0))
                ps = bank[bi]
                dve.wait_ge(filled[bi], YB.through(("var", 0), g))
                ts(vs[:], ps[:, 0:T], EPS, None, ALU.add).then_inc(emptied[bi], 1)
                dve.wait_ge(emptied[bi], YB.through(("var", 0), g))
                ts(h.bitcast(I32), vs[:].bitcast(I32), 1, None, ALU.logical_shift_right).then_inc(newton.sem, 1)
                dve.wait_ge(newton.sem, newton.after(g, 1))
                ts(y.bitcast(I32), h.bitcast(I32), -1.0, float(0x5F3759DF), ALU.mult, ALU.add).then_inc(newton.sem, 1)
                for n in range(3):
                    dve.wait_ge(newton.sem, newton.after(g, 3 * n + 2))
                    tt(h, y, y, ALU.mult).then_inc(newton.sem, 1)
                    dve.wait_ge(newton.sem, newton.after(g, 3 * n + 3))
                    stt(out=h, in0=h, scalar=-0.5, in1=vs[:], op0=ALU.mult, op1=ALU.mult).then_inc(newton.sem, 1)
                    dve.wait_ge(newton.sem, newton.after(g, 3 * n + 4))
                    stt(out=y, in0=h, scalar=1.5, in1=y, op0=ALU.add, op1=ALU.mult).then_inc(newton.sem, 1)

            def groupnorm(g, _):
                pair = [slice(0, 2), slice(2, 4)]
                for p in range(2):
                    bi = YB.of(("spread", p))
                    ps = bank[bi]
                    dve.wait_ge(filled[bi], YB.through(("spread", p), g))
                    tt(att[:, pair[p], :], att[:, pair[p], :], ps[:].rearrange("p (c n) -> p c n", c=2),
                       ALU.mult).then_inc(emptied[bi], 1)
                for p in range(2):
                    dve.wait_ge(emptied[YB.of(("spread", p))], YB.through(("spread", p), g))
                    for c in (2 * p, 2 * p + 1):
                        last = ts(att[:, c, :], att[:, c, :], col("gn_w", c), col("gn_b", c), ALU.mult, ALU.add)
                    last.then_inc(gn_af.sem, 1)
                for p in range(2):
                    dve.wait_ge(gn_af.sem, gn_af.after(g, p + 1))
                    dve.wait_ge(emptied[XB.of(("proj", 8 + p))], XB.through(("proj", 8 + p), g))
                    stt(out=att[:, pair[p], :], in0=gT[:, pair[p], :], scalar=0.5, in1=att[:, pair[p], :],
                        op0=ALU.mult, op1=ALU.mult).then_inc(gated.sem, 1)

            def out_(g, b):
                if b == 0:
                    dve.wait_ge(kept.sem, kept.after(g, NB))
                bi = YB.of(("out", b))
                ps = bank[bi]
                dve.wait_ge(filled[bi], YB.through(("out", b), g))
                tt(keep[:, b, :], ps[:], keep[:, b, :], ALU.add).then_inc(emptied[bi], 1)

            def norm2(g, _):
                dve.wait_ge(emptied[YB.of(("out", 1))], YB.through(("out", 1), g))
                dve.wait_ge(squared.sem, squared.after(g, 2))
                layernorm(g, 2, keep, ln2, EPS)
                dve.wait_ge(row_kept.sem, row_kept.after(g, 1))
                nc.vector.tensor_copy(mnT[:, :, :, 0], prev2[:]).then_inc(rows2.sem, 1)

            def shift2(g, _):
                dve.wait_ge(emptied[YB.of(("turn_m", 1))], YB.through(("turn_m", 1), g))
                dve.wait_ge(rows2.sem, rows2.after(g, 1))
                tt(sx2[:], mnT[:, :, :, 0:L], mnT[:, :, :, 1:], ALU.subtract).then_inc(shifted2.sem, 1)
                dve.wait_ge(shifted2.sem, shifted2.after(g, 1))
                for dst, name, sig in ((xk, "mk", mixk), (xr, "mr", mixr)):
                    for c in range(NC):
                        stt(out=dst[:, c], in0=sx2[:, c], scalar=col(name, c), in1=mnT[:, c, :, 1:],
                            op0=ALU.mult, op1=ALU.add).then_inc(sig.sem, 1)

            def ffn_v(g, b):
                dve.wait_ge(emptied[YB.of(("ffn_r", b))], YB.through(("ffn_r", b), g))
                bi = YB.of(("ffn_v", b))
                ps = bank[bi]
                dve.wait_ge(filled[bi], YB.through(("ffn_v", b), g))
                stt(out=rr[:, b, :], in0=rr[:, b, :], scalar=1.0, in1=ps[:], op0=ALU.add,
                    op1=ALU.mult).then_inc(emptied[bi], 1)
                dve.wait_ge(emptied[YB.of(("ffn_v", b))], YB.through(("ffn_v", b), g))
                stt(out=keep[:, b, :], in0=rr[:, b, :], scalar=0.5, in1=keep[:, b, :], op0=ALU.mult,
                    op1=ALU.add).then_inc(final.sem, 1)

            BD = dict(norm0=norm0, norm1=norm1, shift=shift, mix=mix, keep=keep_row, proj=proj, mean=mean, var=var, groupnorm=groupnorm,
                      out=out_, norm2=norm2, shift2=shift2, ffn_v=ffn_v)

            def db(gd, gb):
                for sec, name, n in DB_STEPS:
                    g = gd if sec == "D" else gb
                    if g is not None and name in BD:
                        BD[name](g, n)

            sections(dve, ca, db)


def kernel(**inputs):
    import numpy as np
    import concourse.bacc as bacc
    from concourse.bass_utils import run_bass_kernel_spmd

    a = {n: np.asarray(v) for n, v in inputs.items()}
    L0 = {n[9:]: v for n, v in a.items() if n.startswith("L0_xattn_")}
    L1 = {n[9:]: v for n, v in a.items() if n.startswith("L1_xattn_")}

    def by_chunk(v):
        return v.reshape(-1, P).T

    def values_first(m):
        s = m.shape[:-1]
        return np.swapaxes(m.reshape(*s, NC, HC, HD), -1, -2).reshape(*s, E)

    def query_order(m):
        s = m.shape[:-1]
        return np.swapaxes(m.reshape(*s, KVH, GRP, HD), -3, -2).reshape(*s, E)

    columns = np.concatenate([
        by_chunk(query_order(L0["bq"])), by_chunk(L0["bk"]), by_chunk(L1["ln1_w"]), by_chunk(L1["ln1_b"]),
        by_chunk(L1["ln2_w"]), by_chunk(L1["ln2_b"]), by_chunk(L1["maa_x"]),
        *[by_chunk(L1["maa_stack"][f]) for f in range(5)], by_chunk(L1["time_decay"]),
        by_chunk(L1["faaaa"].reshape(E)), by_chunk(values_first(L1["gn_w"])), by_chunk(values_first(L1["gn_b"])),
        by_chunk(L1["ffn_maa_k"]), by_chunk(L1["ffn_maa_r"])], axis=1)
    rows = np.concatenate([L0["bo"], L0["gamma"], L0["beta"], L0["bv"]])[None]

    f = np.float32
    p = np.arange(P)
    ident = np.eye(P, dtype=f)
    meanb = (p[:, None] % HC == p[None] % HC).astype(f) / f(HD)
    headb = (p[:, None] // HD == p[None] % HC).astype(f)
    parity = (p[:, None] // HD % 2 == np.arange(2)[None]).astype(f)
    ebase = (p[:, None] // HD == np.arange(56)[None] - 24).astype(f)
    consts = np.concatenate([ident, meanb, headb, parity, ebase], axis=1)
    sel = (p[:, None, None] == np.arange(HD)[None, :, None] * HC + p[None, None] // HD).astype(f)

    bsel = (p[:, None, None] == 32 * np.arange(NC)[None, :, None] + p[None, None] % HC).astype(f)

    host = {
        "x": a["x"], "ctx": a["ctx_2048"], "mask": a["mask_Bx1xSxS2_ff0"],
        "consts": consts, "columns": columns, "rows": rows, "sel": sel, "bsel": bsel,
        "wq": query_order(L0["Wq"]), "wk": L0["Wk"], "wv": L0["Wv"], "wo": query_order(L0["Wo"].T).T,
        "w1": L1["maa_w1"], "w2": L1["maa_w2"].reshape(5 * MAA, E), "dw1": L1["decay_w1"], "dw2": L1["decay_w2"],
        "wr": L1["Wr"].T, "wkk": L1["Wk"].T, "wvv": values_first(L1["Wv"].T), "wg": values_first(L1["Wg"].T),
        "wo2": values_first(L1["Wo"]).T, "fk": L1["ffn_Wk"].T, "fr": L1["ffn_Wr"].T, "fv": L1["ffn_Wv"].T,
    }
    nc = bacc.Bacc("TRN2", target_bir_lowering=False, num_devices=1, dynamic_dma_scratch_size=1024)
    arrays, ap = {}, {}
    for name, v in host.items():
        v = np.ascontiguousarray(v)
        arrays[f"in_{name}"] = v
        ap[name] = nc.dram_tensor(f"in_{name}", v.shape, mybir.dt.from_np(v.dtype), kind="ExternalInput").ap()
    out = nc.dram_tensor("out", (B, L, E), F32, kind="ExternalOutput").ap()
    weights = {n: ap[n] for n in host if n not in ("x", "ctx", "mask")}
    build(nc, ap["x"], ap["ctx"], ap["mask"], weights, out)
    r = run_bass_kernel_spmd(nc, [arrays], core_ids=[0])
    return r.results[0]["out"]
```

```python
from contextlib import ExitStack

import concourse.bass as bass
from concourse import mybir

P = 128
B, L, E = 32, 128, 512
NC = E // P
NB = 2
G = B // NB
T = NB * L
KVH, NH, HD = 8, 32, 16
GRP = NH // KVH
HC = P // HD
MAA, DEC = 32, 64
EPS0, EPS = 1e-6, 1e-5
BIG = 3.4e38

F32 = mybir.dt.float32
I32 = mybir.dt.int32
F32R = mybir.dt.float32r
ALU = mybir.AluOpType
ACT = mybir.ActivationFunctionType

COLS = {}
for _n, _w in (("bq", 4), ("bk", 1), ("ln1_w", 4), ("ln1_b", 4), ("ln2_w", 4), ("ln2_b", 4), ("maa_x", 4),
               ("maa", 20), ("td", 4), ("u", 4), ("gn_w", 4), ("gn_b", 4), ("mk", 4), ("mr", 4)):
    COLS[_n] = (sum(w for _, w in COLS.values()), _w)
NCOL = sum(w for _, w in COLS.values())

MIX = [1, 3, 0, 2, 4]
UNIT_D = [0, 4, 1, 5, 2, 6, 3, 7]
UNITS = NC * len(UNIT_D)
SLOTS = 6
SCORES = NB * 2 * NC


class Signal:

    def __init__(self, sem, per, by=1):
        self.sem, self.per, self.by = sem, per, by

    def after(self, g, n):
        return (g * self.per + n) * self.by


class Banks:

    def __init__(self, jobs):
        self.place, self.uses = {}, {}
        for key, bank in jobs:
            n = self.uses.get(bank, 0)
            self.place[key] = (bank, n)
            self.uses[bank] = n + 1

    def of(self, key):
        return self.place[key][0]

    def earlier(self, key, g):
        k, n = self.place[key]
        return g * self.uses[k] + n

    def through(self, key, g):
        return self.earlier(key, g) + 1


def due(value):
    return not isinstance(value, int) or value > 0


def ring(jobs, banks):
    return [(key, banks[n % len(banks)]) for n, key in enumerate(jobs)]


def attention_slots():
    slots = {}

    def at(s, *step):
        slots.setdefault(s, []).append(step)

    at(0, "turn_c", 0), at(0, "turn_c", 1), at(1, "key", 0), at(2, "value", 0)
    at(3, "turn_x", 0), at(3, "turn_x", 1), at(4, "query", 0), at(5, "query", 1)
    for n in range(SCORES):
        s = 6 + n // 2
        at(s, "score", n)
        at(s + 1, "norm", n)
        at(s + 2, "turn_p", n)
        if n % 4 == 3:
            k = n // 4
            at(s + 3, "values", k)
            if k % 2:
                at(s + 3, "gather", k // 2)
                at(s + 4, "project", k // 2)
                for name, after in (("norm0", 5), ("apply0", 6), ("affine0", 6), ("norm1", 8), ("apply1", 9)):
                    at(s + after, name, k // 2)
    return [slots.get(s, []) for s in range(max(slots) + 1)]


A_SLOTS = attention_slots()
EARLY = 14
CA_SLOTS = max(len(A_SLOTS) + EARLY, UNITS + 6)


def slots_of_a(s):
    return A_SLOTS[s - EARLY] if s - EARLY < len(A_SLOTS) else []


DB_STEPS = [("D", "mean", 0), ("B", "turn_n", 0), ("B", "turn_n", 1), ("D", "mean", 1), ("B", "shift", 0),
            ("D", "var", 0), ("B", "low", 0), ("D", "spread", 0), ("D", "spread", 1), ("D", "groupnorm", 0),
            ("B", "mix", 0), ("B", "mix", 1), ("D", "out", 0), ("B", "proj", 0), ("D", "out", 1),
            ("B", "mix", 2), ("B", "proj", 1), ("D", "norm2", 0), ("B", "mix", 3), ("D", "norm2", 1),
            ("D", "apply2", 0), ("D", "apply2", 1), ("B", "proj", 2), ("B", "mix", 4), ("B", "proj", 3),
            ("C", "unit", 0), ("D", "turn_m", 0), ("D", "turn_m", 1), ("C", "unit", 1), ("D", "shift2", 0),
            ("B", "proj", 4), ("C", "unit", 2), ("C", "unit", 3), ("D", "ffn_k", 0), ("C", "unit", 4),
            ("C", "unit", 5), ("D", "ffn_k", 1), ("C", "unit", 6), ("C", "unit", 7), ("D", "ffn_r", 0),
            ("C", "unit", 8), ("C", "unit", 9), ("D", "ffn_r", 1), ("C", "unit", 10), ("D", "ffn_v", 0),
            ("C", "unit", 11), ("D", "ffn_v", 1), ("C", "unit", 12), ("B", "keep", 0), ("C", "unit", 13)]




NO_PRODUCT = ("norm", "values", "gather", "norm0", "apply0", "affine0", "norm1", "apply1", "shift")


def x_jobs():
    a = [(s[0], s[1]) for slot in A_SLOTS for s in slot if s[0] not in NO_PRODUCT]
    b = []
    for sec, name, n in DB_STEPS:
        if sec == "B" and name in ("turn_n", "low"):
            b += [(name, n)]
        if sec == "B" and name == "mix":
            b += [("mix", 2 * n), ("mix", 2 * n + 1)]
        if sec == "B" and name == "proj":
            b += [("tdecay", 0)] if n == 0 else []
            b += [("proj", 2 * n), ("proj", 2 * n + 1)]
    return ring(a + b, [0, 1, 2, 4])


def y_jobs():
    c = [(("state_v", u), 5 + u % 2) for u in range(UNITS)] + [(("readout", h), 7) for h in range(NC)]
    d = [(name, n) for sec, name, n in DB_STEPS if sec == "D" and name not in ("groupnorm", "norm2", "apply2", "shift2")]
    late = [job for job in d if job[0] not in ("mean", "var", "spread")]
    return c + ring([job for job in d if job not in late], [5, 6, 7]) + ring(late, [3])


def build(nc, x, ctx, mask, w, out):
    XB, YB = Banks(x_jobs()), Banks(y_jobs())
    ctxs = ExitStack()
    with ctxs:
        def sb(name, shape):
            return ctxs.enter_context(nc.sbuf_tensor(name, [P] + list(shape), F32))

        def sem(name):
            return ctxs.enter_context(nc.semaphore(name))

        wq, wk, wv, wo = sb("wq", [NC, E]), sb("wk", [NC, P]), sb("wv", [NC, P]), sb("wo", [NC, E])
        w1, w2s, dw1 = sb("w1", [NC, 5 * MAA]), sb("w2s", [E]), sb("dw1", [NC, DEC])
        low2 = sb("low2", [E])
        big = {n: sb(n, [NC, E]) for n in ("wr", "wkk", "wvv", "wg", "wo2", "fk", "fr", "fv")}
        rows = sb("rows", [3 * E + P])
        bo_r, gam_r, bet_r, bv_r = (rows[:, 0:E], rows[:, E:2 * E], rows[:, 2 * E:3 * E], rows[:, 3 * E:])
        cols = sb("cols", [NCOL])
        consts = sb("consts", [P + P + P + 2 + 56])
        ident, meanb, headb = consts[:, 0:P], consts[:, P:2 * P], consts[:, 2 * P:3 * P]
        parity, ebase = consts[:, 3 * P:3 * P + 2], consts[:, 3 * P + 2:3 * P + 58]
        sel = ctxs.enter_context(nc.sbuf_tensor("sel", [P, HD, P], F32R))
        ublk = sb("ublk", [NC, P])
        bsel = sb("bsel", [NC, P])
        mhalf = sb("mhalf", [NB])
        bqn, bkm = sb("bqn", [NC]), sb("bkm", [2])

        def col(name, c):
            o = COLS[name][0] + c
            return cols[:, o:o + 1]

        xin, keep = sb("xin", [NB, E]), sb("keep", [NB, E])
        cin, nmask, s0 = sb("cin", [NB, E]), sb("nmask", [NB, L]), sb("s0", [NC, NB, HD])
        kbd, vpad = sb("kbd", [NB, KVH, L]), sb("vpad", [NB, KVH, 32])
        prev, prev2 = sb("prev", [NC, NB, 2]), sb("prev2", [NC, NB])
        least, rsum, rinv = sb("least", [SCORES, 4]), sb("rsum", [SCORES, 4]), sb("rinv", [SCORES, 4])
        stats, aggr, rstd = sb("stats", [3, NB, 6]), sb("aggr", [3, NB, 2]), sb("rstd", [3, NB])
        th, th5 = sb("th", [4, T]), sb("th5", [T])
        rT, kT, gT = sb("rT", [NC, T]), sb("kT", [NC, T]), sb("gT", [NC, T])
        v_hi = ctxs.enter_context(nc.sbuf_tensor("v_hi", [P, NC, T], F32R))
        v_lo = ctxs.enter_context(nc.sbuf_tensor("v_lo", [P, NC, T], F32R))
        ws = sb("ws", [NC, NB, L])
        st = sb("st", [SLOTS, 2 * T])
        rk, dg = sb("rk", [2, T]), sb("dg", [2, T])
        att = sb("att", [NC, T])
        vs = sb("vs", [T])
        U = sb("shared", [8464])
        at = [0]

        def view(n, pattern=None, **k):
            ap = U[:, at[0]:at[0] + n]
            at[0] += n
            assert at[0] <= 8464
            return ap.rearrange(pattern, **k) if pattern else ap

        xT = view(NC * T, "p (c b t) -> p c b t", c=NC, b=NB)
        cT = view(NC * T, "p (c b t) -> p c b t", c=NC, b=NB)
        qT = view(NC * T, "p (c b t) -> p c b t", c=NC, b=NB)
        pr = view(4 * 4 * L, "p (s j t) -> p s j t", s=4, j=4)
        pT = view(4 * NC * L, "p (j c t) -> p j c t", j=4, c=NC)
        oT = view(NB * NC * L, "p (b c t) -> p b c t", b=NB, c=NC)
        at[0] = 0
        lnb = view(NB * E, "p (b e) -> p b e", b=NB)
        xnT = view(NC * NB * (L + 1), "p (c b t) -> p c b t", c=NC, b=NB)
        sx = view(NC * T, "p (c b t) -> p c b t", c=NC, b=NB)
        x5 = view(2 * NC * T, "p (s c b t) -> p s c b t", s=2, c=NC, b=NB)
        dt = view(T)
        mnT = view(NC * NB * (L + 1), "p (c b t) -> p c b t", c=NC, b=NB)
        xk = view(NC * T, "p (c b t) -> p c b t", c=NC, b=NB)
        xr = view(NC * T, "p (c b t) -> p c b t", c=NC, b=NB)
        rr = xk.rearrange("p c b t -> p (c b t)").rearrange("p (b e) -> p b e", b=NB)
        e1 = lnb.rearrange("p b e -> p (b e)").rearrange("p (c b t) -> p c b t", c=NC, b=NB)
        gth = e1
        kk = mnT.rearrange("p c b t -> p (c b t)")[:, 0:NC * T].rearrange("p (c b t) -> p c b t", c=NC, b=NB)
        stf = st.ap().rearrange("p s n -> p (s n)") if hasattr(st, "ap") else st[:].rearrange("p s n -> p (s n)")
        sq = stf[:, 0:NC * T].rearrange("p (c n) -> p c n", c=NC)
        ln2, sx2 = cin, att[:].rearrange("p c (b t) -> p c b t", b=NB)

        bank = [ctxs.enter_context(nc.psum_tensor(f"bank{n}", [P, 512], F32)) for n in range(8)]
        filled = [sem(f"bank{n}_filled") for n in range(8)]
        emptied = [sem(f"bank{n}_emptied") for n in range(8)]

        loaded_w = [sem(f"loaded_w{n}") for n in range(4)]
        loaded_x = Signal(sem("loaded_x"), 1, 16)
        loaded_c = Signal(sem("loaded_c"), 1, 16)
        loaded_m = Signal(sem("loaded_m"), 1, 16)
        loaded_s = Signal(sem("loaded_s"), 1, 16)
        stored = Signal(sem("stored"), NB, 16)
        zeroed = sem("buffers_zeroed")
        derived = sem("constants_derived")
        masked = Signal(sem("mask_negated"), 1)
        biased = Signal(sem("x_plus_bo"), NB)
        exped = Signal(sem("exp_done"), SCORES)
        inverted = Signal(sem("sums_inverted"), SCORES)
        normed = Signal(sem("probs_normed"), SCORES)
        valued = Signal(sem("values_summed"), 4)
        gathered = Signal(sem("attention_gathered"), NB)
        rows_saved = Signal(sem("prev_rows_saved"), 1)
        rows_copied = Signal(sem("prev_row_before_ln1"), 1)
        row_kept = Signal(sem("prev_row_kept"), 1)
        rows2 = Signal(sem("prev_row_before_ln2"), 1)
        st_n = [Signal(sem(f"ln{n}_stats"), NB) for n in range(3)]
        ag_n = [Signal(sem(f"ln{n}_aggr"), NB) for n in range(3)]
        rs_n = [Signal(sem(f"ln{n}_var_eps"), NB) for n in range(3)]
        pw_n = [Signal(sem(f"ln{n}_rstd"), NB) for n in range(3)]
        ap_n = [Signal(sem(f"ln{n}_applied"), NB) for n in range(3)]
        gammad = Signal(sem("gamma_done"), NB)
        betad = Signal(sem("beta_done"), NB)
        shifted = Signal(sem("shifted"), 1)
        mixed0 = Signal(sem("maa_x_mixed"), NC)
        tanhed = Signal(sem("low_tanh"), 1)
        mixed = Signal(sem("mix_done"), 10)
        sel_ready = sem("sel_in_its_type")
        v_rounded = Signal(sem("v_hi_done"), 2)
        v_joined = Signal(sem("v_hi_plus_lo"), NC)
        decayed = Signal(sem("decay_done"), NC)
        kept = Signal(sem("x1_kept"), NB)
        gate_th = Signal(sem("gate_tanh"), 2)
        first = Signal(sem("first_state"), UNITS)
        outer = Signal(sem("outer_done"), UNITS)
        scanned = Signal(sem("scan_done"), UNITS)
        weighed = Signal(sem("state_times_r"), UNITS)
        summed = Signal(sem("state_summed"), UNITS // 2)
        rk_done = Signal(sem("r_times_k"), NC)
        diag = Signal(sem("diag_done"), NC)
        squared = Signal(sem("squared"), 2)
        newton = Signal(sem("newton"), 11)
        gn_af = Signal(sem("gn_affine"), 2)
        gated = Signal(sem("gated"), 2)
        shifted2 = Signal(sem("shifted2"), 1)
        mixk, mixr = Signal(sem("mix_k"), NC), Signal(sem("mix_r"), NC)
        relued = Signal(sem("relu_done"), 2)
        ksq = Signal(sem("relu_squared"), 2)
        rval = Signal(sem("r_times_value"), NB)
        final = Signal(sem("final_done"), NB)

        waits = {e: sem(f"waits_of_{e}") for e in ("dve", "pool")}

        def stand(eng, name):
            eng.sem_inc(waits[name], 1)

        def over(ap, n, axis):
            shape = list(ap.shape)
            return ap.unsqueeze(axis).to_broadcast(shape[:axis] + [n] + shape[axis:])

        xg = x.rearrange("(g b) l e -> g l b e", b=NB)
        cg = ctx.rearrange("(g b) l e -> g l b e", b=NB)
        mg = mask.rearrange("(g b) o l s -> g l (b o) s", b=NB)
        og = out.rearrange("(g b) l e -> g b l e", b=NB)
        sg = ctx.rearrange("(g b) l e -> g b (l e)", b=NB)

        block = ctxs.enter_context(nc.Block())

        @block.sync
        def _(sp):
            def load_c(g):
                if due(XB.through(("turn_c", 1), g - 1)):
                    sp.wait_ge(filled[XB.of(("turn_c", 1))], XB.through(("turn_c", 1), g - 1))
                if due(YB.through(("turn_m", 1), g - 2)):
                    sp.wait_ge(filled[YB.of(("turn_m", 1))], YB.through(("turn_m", 1), g - 2))
                sp.dma_start(cin[:], cg[g]).then_inc(loaded_c.sem, 16)

            def load_m(g):
                if due(XB.through(("score", SCORES - 1), g - 1)):
                    sp.wait_ge(emptied[XB.of(("score", SCORES - 1))], XB.through(("score", SCORES - 1), g - 1))
                sp.dma_start(nmask[:], mg[g]).then_inc(loaded_m.sem, 16)

            def load_x(g):
                if due(kept.after(g, 0)):
                    sp.wait_ge(kept.sem, kept.after(g, 0))
                if due(ap_n[1].after(g, 0)):
                    sp.wait_ge(ap_n[1].sem, ap_n[1].after(g, 0))
                sp.dma_start(xin[:], xg[g]).then_inc(loaded_x.sem, 16)

            def load_s(g):
                if due(first.after(g, 0)):
                    sp.wait_ge(first.sem, first.after(g, 0))
                src = sg[g][:, 2 * E:2 * E + HD * E].rearrange("b (c p d) -> p c b d", c=NC, p=P)
                for c in range(NC):
                    sp.dma_start(s0[:, c], src[:, c]).then_inc(loaded_s.sem, 16)

            def store(g):
                for b in range(NB):
                    sp.wait_ge(final.sem, final.after(g, b + 1))
                    sp.dma_start(og[g][b], keep[:, b]).then_inc(stored.sem, 16)

            def wload(n, dst, src):
                sp.dma_start(dst, src).then_inc(loaded_w[n], 16)

            load_c(0)
            wload(0, consts[:], w["consts"])
            wload(0, cols[:], w["columns"])
            wload(0, rows[:], w["rows"].to_broadcast([P, 3 * E + P]))
            sp.dma_start(xin[:], xg[0]).then_inc(loaded_x.sem, 16)
            for dst, n in ((wk, "wk"), (wv, "wv"), (wq, "wq"), (wo, "wo")):
                wload(1, dst[:], w[n].rearrange("(c p) n -> p c n", p=P))
            sp.dma_start(nmask[:], mg[0]).then_inc(loaded_m.sem, 16)
            wload(2, w1[:], w["w1"].rearrange("(c p) n -> p c n", p=P))
            wload(2, w2s[:], w["w2"][0:P, :])
            wload(2, low2[2 * MAA:3 * MAA, :], w["w2"][P:P + MAA, :])
            wload(2, low2[0:DEC, :], w["dw2"])
            wload(2, dw1[:], w["dw1"].rearrange("(c p) n -> p c n", p=P))
            for n in ("wr", "wkk", "wvv", "wg"):
                wload(2, big[n][:], w[n].rearrange("(c p) n -> p c n", p=P))
            load_s(0)
            wload(3, stf[:, 0:HD * P].rearrange("p (d n) -> p d n", d=HD), w["sel"])
            wload(3, bsel[:], w["bsel"])
            for n in ("wo2", "fk", "fr", "fv"):
                wload(3, big[n][:], w[n].rearrange("(c p) n -> p c n", p=P))
            load_c(1)
            load_m(1)
            load_x(1)

            def turn(i):
                load_m(i + 2)
                load_s(i + 1)
                load_c(i + 2)
                store(i)
                load_x(i + 2)

            turn(0)
            with sp.Fori(1, G - 2) as i:
                turn(i)
            load_s(G - 1)
            store(G - 2)
            store(G - 1)
            if due(stored.after(G, 0)):
                sp.wait_ge(stored.sem, stored.after(G, 0))

        W_COUNT = [3 * 16, 4 * 16, 9 * 16, 6 * 16]

        def sections(eng, ca, db):
            ca(None, 0)
            db(None, 0)
            ca(0, 1)
            db(0, 1)
            with eng.Fori(1, G - 1) as i:
                ca(i, i + 1)
                db(i, i + 1)
            ca(G - 1, None)
            db(G - 1, None)

        @block.tensor
        def _(pe):
            mm, tr = nc.tensor.matmul, nc.tensor.transpose

            def turn_x(g, b):
                if b == 0:
                    pe.wait_ge(loaded_x.sem, loaded_x.after(g, 1))
                bi = XB.of(("turn_x", b))
                ps = bank[bi]
                if due(XB.earlier(("turn_x", b), g)):
                    pe.wait_ge(emptied[bi], XB.earlier(("turn_x", b), g))
                for c in range(NC):
                    last = tr(ps[:, c * P:(c + 1) * P], xin[:, b, c * P:(c + 1) * P], ident)
                last.then_inc(filled[bi], 1)

            def turn_c(g, b):
                if b == 0:
                    pe.wait_ge(loaded_c.sem, loaded_c.after(g, 1))
                bi = XB.of(("turn_c", b))
                ps = bank[bi]
                if due(XB.earlier(("turn_c", b), g)):
                    pe.wait_ge(emptied[bi], XB.earlier(("turn_c", b), g))
                for c in range(NC):
                    last = tr(ps[:, c * P:(c + 1) * P], cin[:, b, c * P:(c + 1) * P], ident)
                last.then_inc(filled[bi], 1)

            def key(g, _):
                pe.wait_ge(emptied[XB.of(("turn_c", 1))], XB.through(("turn_c", 1), g))
                bi = XB.of(("key", 0))
                ps = bank[bi]
                if due(XB.earlier(("key", 0), g)):
                    pe.wait_ge(emptied[bi], XB.earlier(("key", 0), g))
                for c in range(NC):
                    last = mm(ps[:, 0:T], wk[:, c, :], cT[:, c], start=c == 0, stop=c == NC - 1)
                last.then_inc(filled[bi], 1)

            def value(g, _):
                bi = XB.of(("value", 0))
                ps = bank[bi]
                if due(XB.earlier(("value", 0), g)):
                    pe.wait_ge(emptied[bi], XB.earlier(("value", 0), g))
                for b in range(NB):
                    for c in range(NC):
                        last = mm(ps[:, b * P:(b + 1) * P], cT[:, c, b, :], wv[:, c, :],
                                  start=c == 0, stop=c == NC - 1)
                last.then_inc(filled[bi], 1)

            def query(g, p):
                if p == 0:
                    pe.wait_ge(emptied[XB.of(("turn_x", 1))], XB.through(("turn_x", 1), g))
                bi = XB.of(("query", p))
                ps = bank[bi]
                if due(XB.earlier(("query", p), g)):
                    pe.wait_ge(emptied[bi], XB.earlier(("query", p), g))
                for q in range(2):
                    c = 2 * p + q
                    for e in range(NC):
                        last = mm(ps[:, q * T:(q + 1) * T], wq[:, e, c * P:(c + 1) * P], xT[:, e],
                                  start=e == 0, stop=e == NC - 1)
                last.then_inc(filled[bi], 1)

            def score(g, n):
                b, half, c = n // 8, n // 4 % 2, n % 4
                if n == 0:
                    pe.wait_ge(emptied[XB.of(("key", 0))], XB.through(("key", 0), g))
                if n in (0, 2):
                    pe.wait_ge(emptied[XB.of(("query", n // 2))], XB.through(("query", n // 2), g))
                bi = XB.of(("score", n))
                ps = bank[bi]
                if due(XB.earlier(("score", n), g)):
                    pe.wait_ge(emptied[bi], XB.earlier(("score", n), g))
                mm(ps[:], qT[:, c, b, :], kbd[:, b, 4 * half:4 * half + 4, :],
                   start=True, stop=True).then_inc(filled[bi], 1)

            def turn_p(g, n):
                pe.wait_ge(normed.sem, normed.after(g, n + 1))
                bi = XB.of(("turn_p", n))
                ps = bank[bi]
                if due(XB.earlier(("turn_p", n), g)):
                    pe.wait_ge(emptied[bi], XB.earlier(("turn_p", n), g))
                for j in range(4):
                    last = tr(ps[:, j * P:(j + 1) * P], pr[:, n % 4, j, :], ident)
                last.then_inc(filled[bi], 1)

            def values(g, k):
                b, half = k // 2, k % 2
                pe.wait_ge(emptied[XB.of(("turn_p", 4 * k + 3))], XB.through(("turn_p", 4 * k + 3), g))
                if k == 0:
                    pe.wait_ge(emptied[XB.of(("value", 0))], XB.through(("value", 0), g))
                if half == 0:
                    if due(gathered.after(g, b)):
                        pe.wait_ge(gathered.sem, gathered.after(g, b))
                for j in (0, 2, 1, 3):
                    h = 4 * half + j
                    r = 32 * (h // 2)
                    last = mm(bank[3][r:r + 32, :], vpad[:, b, h, :], pT[:, j], start=h % 2 == 0, stop=h % 2 == 1)
                last.then_inc(valued.sem, 1)

            def project(g, b):
                pe.wait_ge(gathered.sem, gathered.after(g, b + 1))
                bi = XB.of(("project", b))
                ps = bank[bi]
                if due(XB.earlier(("project", b), g)):
                    pe.wait_ge(emptied[bi], XB.earlier(("project", b), g))
                for c in range(NC):
                    last = mm(ps[:], oT[:, b, c, :], wo[:, c, :], start=c == 0, stop=c == NC - 1)
                last.then_inc(filled[bi], 1)

            A = dict(turn_x=turn_x, turn_c=turn_c, key=key, value=value, query=query, score=score,
                     turn_p=turn_p, values=values, project=project)

            def spread(g, u):
                h, d = u // 8, UNIT_D[u % 8]
                if u == 0:
                    pe.wait_ge(emptied[XB.of(("proj", 7))], XB.through(("proj", 7), g))
                bi = YB.of(("state_v", u))
                ps = bank[bi]
                if due(YB.earlier(("state_v", u), g)):
                    pe.wait_ge(emptied[bi], YB.earlier(("state_v", u), g))
                for q in range(2):
                    mm(ps[:, q * T:(q + 1) * T], sel[:, d + 8 * q, :], v_hi[:, h, :], start=True, stop=False)
                    last = mm(ps[:, q * T:(q + 1) * T], sel[:, d + 8 * q, :], v_lo[:, h, :],
                              start=False, stop=True)
                last.then_inc(filled[bi], 1)

            def bonus(g, h):
                pe.wait_ge(rk_done.sem, rk_done.after(g, h + 1))
                bi = YB.of(("readout", h))
                ps = bank[bi]
                if due(YB.earlier(("readout", h), g)):
                    pe.wait_ge(emptied[bi], YB.earlier(("readout", h), g))
                mm(ps[:, T:2 * T], ublk[:, h, :], rk[:, h % 2, :], start=True, stop=True).then_inc(filled[bi], 1)

            def reduce(g, q):
                m, h = q % 4, q // 4
                if m == 0:
                    bonus(g, h)
                pe.wait_ge(weighed.sem, weighed.after(g, 2 * q + 2))
                ps = bank[7]
                for u in (2 * q, 2 * q + 1):
                    for s in range(2):
                        d = UNIT_D[u % 8] + 8 * s
                        o = 24 - 8 * (d % 4)
                        last = mm(ps[32 * (d // 4):32 * (d // 4) + 32, 0:T], ebase[:, o:o + 32],
                                  st[:, u % SLOTS, s * T:(s + 1) * T], start=m == 0, stop=m == 3)
                last.then_inc(summed.sem, 1)

            def unit(g, s):
                if s < UNITS:
                    spread(g, s)
                if s >= 4 and s % 2 == 0 and (s - 4) // 2 < UNITS // 2:
                    reduce(g, (s - 4) // 2)

            def ca(gc, ga):
                if gc is None:
                    pe.wait_ge(loaded_w[0], W_COUNT[0])
                for s in range(EARLY, CA_SLOTS):
                    if gc is not None:
                        unit(gc, s)
                    if ga is not None:
                        for name, n in slots_of_a(s):
                            if gc is None and name == "key":
                                pe.wait_ge(loaded_w[1], W_COUNT[1])
                            if name in A:
                                A[name](ga, n)
                            elif name in BD:
                                BD[name](ga, n)

            def turn_n(g, p):
                pe.wait_ge(ap_n[1].sem, ap_n[1].after(g, NB))
                bi = XB.of(("turn_n", p))
                ps = bank[bi]
                if due(XB.earlier(("turn_n", p), g)):
                    pe.wait_ge(emptied[bi], XB.earlier(("turn_n", p), g))
                for q in range(2):
                    for b in range(NB):
                        c = 2 * p + q
                        o = q * T + b * P
                        last = tr(ps[:, o:o + P], lnb[:, b, c * P:(c + 1) * P], ident)
                last.then_inc(filled[bi], 1)

            def low(g, _):
                pe.wait_ge(mixed0.sem, mixed0.after(g, NC))
                bi = XB.of(("low", 0))
                ps = bank[bi]
                if due(XB.earlier(("low", 0), g)):
                    pe.wait_ge(emptied[bi], XB.earlier(("low", 0), g))
                for c in range(NC):
                    mm(ps[:, 0:T], w1[:, c, 0:P], x5[:, 0, c], start=c == 0, stop=c == NC - 1)
                for c in range(NC):
                    last = mm(ps[64:96, T:2 * T], w1[:, c, P:P + MAA], x5[:, 0, c], start=c == 0, stop=c == NC - 1)
                last.then_inc(filled[bi], 1)

            def mix(g, k):
                f = MIX[k]
                if k == 0:
                    pe.wait_ge(tanhed.sem, tanhed.after(g, 1))
                for p in range(2):
                    bi = XB.of(("mix", 2 * k + p))
                    ps = bank[bi]
                    if due(XB.earlier(("mix", 2 * k + p), g)):
                        pe.wait_ge(emptied[bi], XB.earlier(("mix", 2 * k + p), g))
                    for q in range(2):
                        c = 2 * p + q
                        if f < 4:
                            last = mm(ps[:, q * T:(q + 1) * T], w2s[:, c * P:(c + 1) * P], th[:, f, :],
                                      start=True, stop=True)
                        else:
                            last = mm(ps[:, q * T:(q + 1) * T], low2[64:96, c * P:(c + 1) * P], th5[64:96, :],
                                      start=True, stop=True)
                    last.then_inc(filled[bi], 1)

            def proj(g, k):
                pe.wait_ge(mixed.sem, mixed.after(g, 2 * k + 2))
                if k == 0:
                    bi = XB.of(("tdecay", 0))
                    ps = bank[bi]
                    if due(XB.earlier(("tdecay", 0), g)):
                        pe.wait_ge(emptied[bi], XB.earlier(("tdecay", 0), g))
                    for c in range(NC):
                        last = mm(ps[0:DEC, 0:T], dw1[:, c, :], x5[:, 0, c], start=c == 0, stop=c == NC - 1)
                    last.then_inc(filled[bi], 1)
                    pe.wait_ge(emptied[XB.of(("tdecay", 0))], XB.through(("tdecay", 0), g))
                    for p in range(2):
                        bi = XB.of(("proj", p))
                        ps = bank[bi]
                        if due(XB.earlier(("proj", p), g)):
                            pe.wait_ge(emptied[bi], XB.earlier(("proj", p), g))
                        for q in range(2):
                            c = 2 * p + q
                            last = mm(ps[:, q * T:(q + 1) * T], low2[0:DEC, c * P:(c + 1) * P], dt[0:DEC, :],
                                      start=True, stop=True)
                        last.then_inc(filled[bi], 1)
                    return
                wt = big[("wr", "wkk", "wvv", "wg")[k - 1]]
                for p in range(2):
                    bi = XB.of(("proj", 2 * k + p))
                    ps = bank[bi]
                    if due(XB.earlier(("proj", 2 * k + p), g)):
                        pe.wait_ge(emptied[bi], XB.earlier(("proj", 2 * k + p), g))
                    for q in range(2):
                        c = 2 * p + q
                        for e in range(NC):
                            last = mm(ps[:, q * T:(q + 1) * T], wt[:, e, c * P:(c + 1) * P], x5[:, k % 2, e],
                                      start=e == 0, stop=e == NC - 1)
                    last.then_inc(filled[bi], 1)

            def mean(g, p):
                pe.wait_ge(emptied[YB.of(("readout", 2 * p + 1))], YB.through(("readout", 2 * p + 1), g))
                bi = YB.of(("mean", p))
                ps = bank[bi]
                if due(YB.earlier(("mean", p), g)):
                    pe.wait_ge(emptied[bi], YB.earlier(("mean", p), g))
                for q in range(2):
                    last = mm(ps[:, q * T:(q + 1) * T], meanb, att[:, 2 * p + q, :], start=True, stop=True)
                last.then_inc(filled[bi], 1)

            def var(g, _):
                pe.wait_ge(squared.sem, squared.after(g, 2))
                bi = YB.of(("var", 0))
                ps = bank[bi]
                if due(YB.earlier(("var", 0), g)):
                    pe.wait_ge(emptied[bi], YB.earlier(("var", 0), g))
                for c in range(NC):
                    last = mm(ps[32 * c:32 * c + 32, 0:T], meanb[:, 0:32], sq[:, c, :], start=True, stop=True)
                last.then_inc(filled[bi], 1)

            def spread_rstd(g, p):
                pe.wait_ge(newton.sem, newton.after(g, 11))
                bi = YB.of(("spread", p))
                ps = bank[bi]
                if due(YB.earlier(("spread", p), g)):
                    pe.wait_ge(emptied[bi], YB.earlier(("spread", p), g))
                for q in range(2):
                    last = mm(ps[:, q * T:(q + 1) * T], bsel[:, 2 * p + q, :], dg[:, 0, :], start=True, stop=True)
                last.then_inc(filled[bi], 1)

            def out_(g, b):
                pe.wait_ge(gated.sem, gated.after(g, 2))
                bi = YB.of(("out", b))
                ps = bank[bi]
                if due(YB.earlier(("out", b), g)):
                    pe.wait_ge(emptied[bi], YB.earlier(("out", b), g))
                for c in range(NC):
                    last = mm(ps[:], att[:, c, b * P:(b + 1) * P], big["wo2"][:, c, :], start=c == 0, stop=c == NC - 1)
                last.then_inc(filled[bi], 1)

            def turn_m(g, p):
                pe.wait_ge(ap_n[2].sem, ap_n[2].after(g, NB))
                bi = YB.of(("turn_m", p))
                ps = bank[bi]
                if due(YB.earlier(("turn_m", p), g)):
                    pe.wait_ge(emptied[bi], YB.earlier(("turn_m", p), g))
                for q in range(2):
                    for b in range(NB):
                        c = 2 * p + q
                        o = q * T + b * P
                        last = tr(ps[:, o:o + P], ln2[:, b, c * P:(c + 1) * P], ident)
                last.then_inc(filled[bi], 1)

            def ffn_k(g, p):
                pe.wait_ge(mixk.sem, mixk.after(g, NC))
                bi = YB.of(("ffn_k", p))
                ps = bank[bi]
                if due(YB.earlier(("ffn_k", p), g)):
                    pe.wait_ge(emptied[bi], YB.earlier(("ffn_k", p), g))
                for q in range(2):
                    c = 2 * p + q
                    for e in range(NC):
                        last = mm(ps[:, q * T:(q + 1) * T], big["fk"][:, e, c * P:(c + 1) * P], xk[:, e],
                                  start=e == 0, stop=e == NC - 1)
                last.then_inc(filled[bi], 1)

            def ffn_r(g, b):
                pe.wait_ge(mixr.sem, mixr.after(g, NC))
                bi = YB.of(("ffn_r", b))
                ps = bank[bi]
                if due(YB.earlier(("ffn_r", b), g)):
                    pe.wait_ge(emptied[bi], YB.earlier(("ffn_r", b), g))
                for c in range(NC):
                    last = mm(ps[:], xr[:, c, b, :], big["fr"][:, c, :], start=c == 0, stop=c == NC - 1)
                last.then_inc(filled[bi], 1)

            def ffn_v(g, b):
                pe.wait_ge(ksq.sem, ksq.after(g, 2))
                bi = YB.of(("ffn_v", b))
                ps = bank[bi]
                if due(YB.earlier(("ffn_v", b), g)):
                    pe.wait_ge(emptied[bi], YB.earlier(("ffn_v", b), g))
                for c in range(NC):
                    last = mm(ps[:], kk[:, c, b, :], big["fv"][:, c, :], start=c == 0, stop=c == NC - 1)
                last.then_inc(filled[bi], 1)

            BD = dict(turn_n=turn_n, low=low, mix=mix, proj=proj, mean=mean, var=var, spread=spread_rstd, out=out_, turn_m=turn_m,
                      ffn_k=ffn_k, ffn_r=ffn_r, ffn_v=ffn_v)

            BD["unit"] = unit

            def db(gd, gb):
                for sec, name, n in DB_STEPS:
                    if gd is None and name == "low":
                        pe.wait_ge(loaded_w[2], W_COUNT[2])
                        pe.wait_ge(zeroed, 1)
                        pe.wait_ge(derived, 1)
                    if gd is None and (name, n) == ("unit", 0):
                        pe.wait_ge(loaded_w[3], W_COUNT[3])
                        pe.wait_ge(sel_ready, 1)
                    g = gd if sec == "D" else gb
                    if g is not None and name in BD:
                        BD[name](g, n)

            sections(pe, ca, db)

        @block.scalar
        def _(act):
            fn = nc.scalar.activation

            def evac_turn(name, dst):
                def step(g, b):
                    if b == 0 and name == "turn_c":
                        if due(XB.through(("proj", 9), g - 1)):
                            act.wait_ge(emptied[XB.of(("proj", 9))], XB.through(("proj", 9), g - 1))
                    bi = XB.of((name, b))
                    ps = bank[bi]
                    act.wait_ge(filled[bi], XB.through((name, b), g))
                    fn(dst[:, :, b, :], ps[:].rearrange("p (c t) -> p c t", c=NC), ACT.Copy).then_inc(emptied[bi], 1)
                return step

            def key(g, _):
                if due(XB.through(("score", SCORES - 1), g - 1)):
                    act.wait_ge(emptied[XB.of(("score", SCORES - 1))], XB.through(("score", SCORES - 1), g - 1))
                bi = XB.of(("key", 0))
                ps = bank[bi]
                act.wait_ge(filled[bi], XB.through(("key", 0), g))
                for h in range(KVH):
                    r = slice(32 * (h // 2), 32 * (h // 2) + 32)
                    last = fn(kbd[r, :, h, :], ps[r, 0:T].rearrange("p (b t) -> p b t", b=NB), ACT.Identity,
                              bias=bkm[r, h % 2:h % 2 + 1], scale=parity[r, h % 2:h % 2 + 1])
                last.then_inc(emptied[bi], 1)

            def query(g, p):
                bi = XB.of(("query", p))
                ps = bank[bi]
                act.wait_ge(filled[bi], XB.through(("query", p), g))
                for q in range(2):
                    c = 2 * p + q
                    last = fn(qT[:, c], ps[:, q * T:(q + 1) * T].rearrange("p (b t) -> p b t", b=NB), ACT.Identity,
                              bias=bqn[:, c:c + 1], scale=-0.25)
                last.then_inc(emptied[bi], 1)

            def score(g, n):
                act.wait_ge(emptied[XB.of(("score", n))], XB.through(("score", n), g))
                for j in range(4):
                    last = fn(pr[:, n % 4, j, :], pr[:, n % 4, j, :], ACT.Exp, bias=least[:, n, j:j + 1], scale=-1.0,
                              accum_out=rsum[:, n, j:j + 1])
                last.then_inc(exped.sem, 1)

            def turn_p(g, n):
                if n == 0 and due(final.after(g - 1, 0)):
                    act.wait_ge(final.sem, final.after(g - 1, 0))
                if n % 4 == 0:
                    if due(valued.after(g, n // 4)):
                        act.wait_ge(valued.sem, valued.after(g, n // 4))
                bi = XB.of(("turn_p", n))
                ps = bank[bi]
                act.wait_ge(filled[bi], XB.through(("turn_p", n), g))
                fn(pT[:, :, n % 4, :], ps[:].rearrange("p (j t) -> p j t", j=4), ACT.Copy).then_inc(emptied[bi], 1)

            def gather(g, b):
                act.wait_ge(valued.sem, valued.after(g, 2 * b + 2))
                fn(oT[:, b], bank[3][:].rearrange("p (c t) -> p c t", c=NC), ACT.Copy).then_inc(gathered.sem, 1)

            A = dict(turn_x=evac_turn("turn_x", xT), turn_c=evac_turn("turn_c", cT), key=key, query=query,
                     score=score, turn_p=turn_p, gather=gather)

            def ca(gc, ga):
                if gc is None:
                    act.wait_ge(zeroed, 1)
                    act.wait_ge(derived, 1)
                if ga is None:
                    return
                for slot in A_SLOTS:
                    for name, n in slot:
                        if name in A:
                            A[name](ga, n)
                        elif name in BD:
                            BD[name](ga, n)

            def halves(ps, q):
                return ps[:, q * T:(q + 1) * T].rearrange("p (b t) -> p b t", b=NB)

            def turn_n(g, p):
                bi = XB.of(("turn_n", p))
                ps = bank[bi]
                act.wait_ge(filled[bi], XB.through(("turn_n", p), g))
                for q in range(2):
                    c = 2 * p + q
                    last = fn(xnT[:, c, :, 1:], halves(ps, q), ACT.Identity, bias=col("ln1_b", c),
                              scale=col("ln1_w", c))
                last.then_inc(emptied[bi], 1)

            def low(g, _):
                bi = XB.of(("low", 0))
                ps = bank[bi]
                act.wait_ge(filled[bi], XB.through(("low", 0), g))
                for f in range(4):
                    r = slice(32 * f, 32 * f + 32)
                    fn(th[r, f, :], ps[r, 0:T], ACT.Tanh)
                fn(th5[64:96, :], ps[64:96, T:2 * T], ACT.Tanh).then_inc(emptied[bi], 1)
                act.wait_ge(emptied[XB.of(("low", 0))], XB.through(("low", 0), g))
                act.sem_inc(tanhed.sem, 1)

            def keep_x1(g, _):
                if due(stored.after(g, 0)):
                    act.wait_ge(stored.sem, stored.after(g, 0))
                act.wait_ge(betad.sem, betad.after(g, NB))
                for b in range(NB):
                    fn(keep[:, b, :], xin[:, b, :], ACT.Copy).then_inc(kept.sem, 1)

            def proj(g, k):
                if k == 0:
                    bi = XB.of(("tdecay", 0))
                    ps = bank[bi]
                    act.wait_ge(filled[bi], XB.through(("tdecay", 0), g))
                    fn(dt[0:DEC, :], ps[0:DEC, 0:T], ACT.Tanh).then_inc(emptied[bi], 1)
                    if due(YB.through(("readout", NC - 1), g - 1)):
                        act.wait_ge(emptied[YB.of(("readout", NC - 1))], YB.through(("readout", NC - 1), g - 1))
                for p in range(2):
                    bi = XB.of(("proj", 2 * k + p))
                    ps = bank[bi]
                    act.wait_ge(filled[bi], XB.through(("proj", 2 * k + p), g))
                    if k == 0:
                        for q in range(2):
                            last = fn(e1[:, 2 * p + q], halves(ps, q), ACT.Exp, bias=col("td", 2 * p + q))
                        last.then_inc(emptied[bi], 1)
                        act.wait_ge(emptied[XB.of(("proj", p))], XB.through(("proj", p), g))
                        for q in range(2):
                            c = 2 * p + q
                            fn(ws[:, c, :, 1:], e1[:, c, :, 0:L - 1], ACT.Exp, scale=-1.0).then_inc(decayed.sem, 1)
                    elif k < 4:
                        dst = (rT, kT, v_hi)[k - 1]
                        fn(dst[:, 2 * p:2 * p + 2, :], ps[:].rearrange("p (c n) -> p c n", c=2),
                           ACT.Copy).then_inc(v_rounded.sem if k == 3 else emptied[bi], 1)
                    else:
                        fn(gth[:, 2 * p:2 * p + 2].rearrange("p c b t -> p (c b t)"), ps[:], ACT.Tanh,
                           scale=0.5).then_inc(gate_th.sem, 1)

            def var(g, _):
                for p in range(2):
                    act.wait_ge(emptied[YB.of(("mean", p))], YB.through(("mean", p), g))
                    fn(sq[:, 2 * p:2 * p + 2, :], att[:, 2 * p:2 * p + 2, :], ACT.Square).then_inc(squared.sem, 1)

            def turn_m(g, p):
                bi = YB.of(("turn_m", p))
                ps = bank[bi]
                act.wait_ge(filled[bi], YB.through(("turn_m", p), g))
                for q in range(2):
                    c = 2 * p + q
                    last = fn(mnT[:, c, :, 1:], halves(ps, q), ACT.Identity, bias=col("ln2_b", c),
                              scale=col("ln2_w", c))
                last.then_inc(emptied[bi], 1)

            def ffn_k(g, p):
                bi = YB.of(("ffn_k", p))
                ps = bank[bi]
                act.wait_ge(filled[bi], YB.through(("ffn_k", p), g))
                act.wait_ge(mixr.sem, mixr.after(g, NC))
                v = kk[:, 2 * p:2 * p + 2].rearrange("p c b t -> p (c b t)")
                fn(v, ps[:], ACT.Relu).then_inc(emptied[bi], 1)
                act.wait_ge(emptied[YB.of(("ffn_k", p))], YB.through(("ffn_k", p), g))
                fn(v, v, ACT.Square).then_inc(ksq.sem, 1)

            def ffn_r(g, b):
                bi = YB.of(("ffn_r", b))
                ps = bank[bi]
                act.wait_ge(filled[bi], YB.through(("ffn_r", b), g))
                fn(rr[:, b, :], ps[:], ACT.Tanh, scale=0.5).then_inc(emptied[bi], 1)

            BD = dict(turn_n=turn_n, low=low, keep=keep_x1, proj=proj, var=var, turn_m=turn_m, ffn_k=ffn_k,
                      ffn_r=ffn_r)

            def db(gd, gb):
                for sec, name, n in DB_STEPS:
                    g = gd if sec == "D" else gb
                    if g is not None and name in BD:
                        BD[name](g, n)

            sections(act, ca, db)

        @block.gpsimd
        def _(pool):
            tt = nc.gpsimd.tensor_tensor

            def turn_x(g, b):
                pool.wait_ge(filled[XB.of(("turn_x", b))], XB.through(("turn_x", b), g))
                if b == 0:
                    pool.wait_ge(loaded_x.sem, loaded_x.after(g, 1))
                tt(xin[:, b, :], xin[:, b, :], bo_r, ALU.add).then_inc(biased.sem, 1)

            def negate(g):
                pool.wait_ge(loaded_m.sem, loaded_m.after(g, 1))
                stand(pool, "pool")
                nc.gpsimd.tensor_scalar(nmask[:], nmask[:], -1.0, 0.0, ALU.mult, ALU.add).then_inc(masked.sem, 1)

            def norm(g, n):
                pool.wait_ge(inverted.sem, inverted.after(g, n + 1))
                v = pr[:, n % 4]
                tt(v, v, rinv[:, n, :].unsqueeze(2).to_broadcast([P, 4, L]), ALU.mult).then_inc(normed.sem, 1)

            def first_state(g, u):
                h, d = u // 8, UNIT_D[u % 8]
                if u == 0:
                    pool.wait_ge(loaded_s.sem, loaded_s.after(g * NC, NC))
                    if due(gated.after(g, 0)):
                        pool.wait_ge(gated.sem, gated.after(g, 0))
                if u >= SLOTS:
                    pool.wait_ge(summed.sem, summed.after(g, (u - SLOTS) // 2 + 1))
                if u == 0 or u >= SLOTS:
                    stand(pool, "pool")
                dst = st[:, u % SLOTS, :].rearrange("p (d b t) -> p d b t", d=2, b=NB)[:, :, :, 0]
                src = s0[:, h, :, d:d + 9:8].rearrange("p b d -> p d b")
                nc.gpsimd.tensor_copy(dst, src).then_inc(first.sem, 1)

            def r_times_k(g, h):
                if h == 0:
                    pool.wait_ge(emptied[XB.of(("proj", 5))], XB.through(("proj", 5), g))
                if h >= 2:
                    pool.wait_ge(filled[YB.of(("readout", h - 2))], YB.through(("readout", h - 2), g))
                tt(rk[:, h % 2, :], rT[:, h, :], kT[:, h, :], ALU.mult).then_inc(rk_done.sem, 1)
                if h == 0:
                    pool.wait_ge(emptied[XB.of(("proj", 7))], XB.through(("proj", 7), g))
                if h >= 2:
                    pool.wait_ge(emptied[YB.of(("readout", h - 2))], YB.through(("readout", h - 2), g))
                tt(dg[:, h % 2, :], v_hi[:, h, :].bitcast(F32), v_lo[:, h, :].bitcast(F32),
                   ALU.add).then_inc(v_joined.sem, 1)

            def unit(g, s):
                if s < UNITS:
                    first_state(g, s)
                if s < UNITS and s % 8 == 0:
                    r_times_k(g, s // 8)

            def ca(gc, ga):
                for s in range(EARLY, CA_SLOTS):
                    if gc is not None:
                        unit(gc, s)
                    if ga is not None:
                        if s == EARLY + 2:
                            negate(ga)
                        for name, n in slots_of_a(s):
                            if name == "turn_x":
                                turn_x(ga, n)
                            if name == "norm":
                                norm(ga, n)
                            elif name in BD:
                                BD[name](ga, n)

            def affine0(g, b):
                pool.wait_ge(ap_n[0].sem, ap_n[0].after(g, b + 1))
                tt(xin[:, b, :], xin[:, b, :], gam_r, ALU.mult).then_inc(gammad.sem, 1)
                pool.wait_ge(gammad.sem, gammad.after(g, b + 1))
                tt(xin[:, b, :], xin[:, b, :], bet_r, ALU.add).then_inc(betad.sem, 1)

            def mix(g, k):
                for p in range(2):
                    pool.wait_ge(emptied[XB.of(("mix", 2 * k + p))], XB.through(("mix", 2 * k + p), g))
                    v = x5[:, k % 2, 2 * p:2 * p + 2]
                    tt(v, v, xnT[:, 2 * p:2 * p + 2, :, 1:], ALU.add).then_inc(mixed.sem, 1)

            def inverse_root(n):
                def step(g, b):
                    pool.wait_ge(rs_n[n].sem, rs_n[n].after(g, b + 1))
                    v = rstd[:, n, b:b + 1]
                    tt(v, v, mhalf[:, 0:1], ALU.pow).then_inc(pw_n[n].sem, 1)
                return step

            BD = dict(norm0=inverse_root(0), norm1=inverse_root(1), norm2=inverse_root(2), affine0=affine0, mix=mix,
                      unit=unit)

            def db(gd, gb):
                for sec, name, n in DB_STEPS:
                    if gd is None and (name, n) == ("unit", 0):
                        pool.wait_ge(loaded_w[3], W_COUNT[3])
                        nc.gpsimd.tensor_copy(sel[:], stf[:, 0:HD * P].rearrange(
                            "p (d n) -> p d n", d=HD)).then_inc(sel_ready, 1)
                        pool.wait_ge(sel_ready, 1)
                    g = gd if sec == "D" else gb
                    if g is not None and name in BD:
                        BD[name](g, n)

            nc.gpsimd.memset(kbd[:], 0.0)
            nc.gpsimd.memset(vpad[:], 0.0)
            nc.gpsimd.memset(th[:], 0.0)
            nc.gpsimd.memset(mhalf[:], -0.5)
            nc.gpsimd.memset(ws[:], 0.0).then_inc(zeroed, 1)
            pool.wait_ge(zeroed, 1)
            pool.wait_ge(loaded_w[0], W_COUNT[0])
            sections(pool, ca, db)

        @block.vector
        def _(dve):
            tt, ts, stt = nc.vector.tensor_tensor, nc.vector.tensor_scalar, nc.vector.scalar_tensor_tensor

            def key(g, _):
                dve.wait_ge(emptied[XB.of(("turn_c", 1))], XB.through(("turn_c", 1), g))
                nc.vector.tensor_copy(prev[:], cT[:, :, :, 0:2]).then_inc(rows_saved.sem, 1)

            def value(g, _):
                if due(valued.after(g, 0)):
                    dve.wait_ge(valued.sem, valued.after(g, 0))
                bi = XB.of(("value", 0))
                ps = bank[bi]
                dve.wait_ge(filled[bi], XB.through(("value", 0), g))
                pv = ps[:, 0:T].rearrange("p (b h q d) -> p b h q d", b=NB, q=2, d=HD)
                vp = vpad[:].rearrange("p b (h q) n -> p b h q n", q=2)
                bv = bv_r.rearrange("p (h q d) -> p h q d", q=2, d=HD)
                for q in range(2):
                    last = tt(vp[:, :, :, q, q * HD:(q + 1) * HD], pv[:, :, :, q, :], over(bv[:, :, q, :], NB, 1),
                              ALU.add)
                last.then_inc(emptied[bi], 1)

            def score(g, n):
                if n == 0:
                    dve.wait_ge(masked.sem, masked.after(g, 1))
                    if due(XB.through(("proj", 9), g - 1)):
                        dve.wait_ge(emptied[XB.of(("proj", 9))], XB.through(("proj", 9), g - 1))
                if n >= 4 and XB.of(("turn_p", n - 4)) != XB.of(("score", n)):
                    dve.wait_ge(filled[XB.of(("turn_p", n - 4))], XB.through(("turn_p", n - 4), g))
                bi = XB.of(("score", n))
                ps = bank[bi]
                dve.wait_ge(filled[bi], XB.through(("score", n), g))
                stand(dve, "dve")
                for j in range(4):
                    last = nc.vector.tensor_tensor_reduce(pr[:, n % 4, j, :], ps[:, j * P:(j + 1) * P],
                                                          nmask[:, n // 8, :], 1.0, BIG, ALU.add, ALU.min,
                                                          least[:, n, j:j + 1])
                last.then_inc(emptied[bi], 1)

            def norm(g, n):
                dve.wait_ge(exped.sem, exped.after(g, n + 1))
                nc.vector.reciprocal(rinv[:, n, :], rsum[:, n, :]).then_inc(inverted.sem, 1)

            def project(g, b):
                dve.wait_ge(biased.sem, biased.after(g, b + 1))
                bi = XB.of(("project", b))
                ps = bank[bi]
                dve.wait_ge(filled[bi], XB.through(("project", b), g))
                tt(xin[:, b, :], ps[:], xin[:, b, :], ALU.add).then_inc(emptied[bi], 1)

            A = dict(key=key, value=value, score=score, norm=norm, project=project)

            def outer_(g, u):
                h = u // 8
                if u == 0:
                    dve.wait_ge(emptied[XB.of(("proj", 5))], XB.through(("proj", 5), g))
                    if due(gated.after(g, 0)):
                        dve.wait_ge(gated.sem, gated.after(g, 0))
                if u >= SLOTS:
                    dve.wait_ge(summed.sem, summed.after(g, (u - SLOTS) // 2 + 1))
                bi = YB.of(("state_v", u))
                ps = bank[bi]
                dve.wait_ge(filled[bi], YB.through(("state_v", u), g))
                dst = st[:, u % SLOTS, :].rearrange("p (d b t) -> p d b t", d=2, b=NB)[:, :, :, 1:]
                src = ps[:].rearrange("p (d b t) -> p d b t", d=2, b=NB)[:, :, :, 0:L - 1]
                kv = kT[:, h, :].rearrange("p (b t) -> p b t", b=NB)[:, :, 0:L - 1]
                tt(dst, src, over(kv, 2, 1), ALU.mult).then_inc(emptied[bi], 1)

            def scan(g, u):
                h = u // 8
                if u % 16 == 0:
                    dve.wait_ge(decayed.sem, decayed.after(g, 2 * (u // 16) + 2))
                dve.wait_ge(emptied[YB.of(("state_v", u))], YB.through(("state_v", u), g))
                dve.wait_ge(first.sem, first.after(g, u + 1))
                for s in range(2):
                    v = st[:, u % SLOTS, s * T:(s + 1) * T]
                    last = nc.vector.tensor_tensor_scan(v, ws[:, h].rearrange("p b t -> p (b t)"), v, 0.0,
                                                        ALU.mult, ALU.add)
                last.then_inc(scanned.sem, 1)

            def weigh(g, u):
                dve.wait_ge(scanned.sem, scanned.after(g, u + 1))
                v = st[:, u % SLOTS, :].rearrange("p (d n) -> p d n", d=2)
                tt(v, v, over(rT[:, u // 8, :], 2, 1), ALU.mult).then_inc(weighed.sem, 1)

            def readout(g, h):
                bi = YB.of(("readout", h))
                ps = bank[bi]
                dve.wait_ge(filled[bi], YB.through(("readout", h), g))
                dve.wait_ge(summed.sem, summed.after(g, 4 * h + 4))
                dve.wait_ge(v_joined.sem, v_joined.after(g, h + 1))
                tt(dg[:, h % 2, :], ps[:, T:2 * T], dg[:, h % 2, :], ALU.mult).then_inc(diag.sem, 1)
                dve.wait_ge(diag.sem, diag.after(g, h + 1))
                tt(att[:, h, :], ps[:, 0:T], dg[:, h % 2, :], ALU.add).then_inc(emptied[bi], 1)

            def unit(g, s):
                if s >= 11 and (s - 11) % 8 == 0:
                    readout(g, (s - 11) // 8)
                if s < UNITS:
                    outer_(g, s)
                if 1 <= s <= UNITS:
                    scan(g, s - 1)
                if 2 <= s <= UNITS + 1:
                    weigh(g, s - 2)

            def ca(gc, ga):
                if ga is not None and gc is None:
                    dve.wait_ge(loaded_w[0], W_COUNT[0])
                    o = COLS["bq"][0]
                    ts(bqn[:], cols[:, o:o + NC], -0.25, None, ALU.mult)
                    ts(bkm[:], parity, col("bk", 0), None, ALU.mult)
                    for c in range(NC):
                        last = ts(ublk[:, c, :], headb, col("u", c), None, ALU.mult)
                    last.then_inc(derived, 1)
                    dve.wait_ge(zeroed, 1)
                for s in range(EARLY, CA_SLOTS):
                    if gc is not None:
                        unit(gc, s)
                    if ga is not None:
                        for name, n in slots_of_a(s):
                            if name in A:
                                A[name](ga, n)
                            elif name in BD:
                                BD[name](ga, n)

            def statistics(g, b, n, src, eps):
                nc.vector.bn_stats(stats[:, n, b, :], src[:, b, :]).then_inc(st_n[n].sem, 1)
                dve.wait_ge(st_n[n].sem, st_n[n].after(g, b + 1))
                stand(dve, "dve")
                nc.vector.bn_aggr(aggr[:, n, b, :], stats[:, n, b, :]).then_inc(ag_n[n].sem, 1)
                dve.wait_ge(ag_n[n].sem, ag_n[n].after(g, b + 1))
                ts(rstd[:, n, b:b + 1], aggr[:, n, b, 1:2], eps, None, ALU.add).then_inc(rs_n[n].sem, 1)

            def apply_norm(g, b, n, src, dst):
                dve.wait_ge(pw_n[n].sem, pw_n[n].after(g, b + 1))
                ts(dst[:, b, :], src[:, b, :], aggr[:, n, b, 0:1], rstd[:, n, b:b + 1], ALU.subtract,
                   ALU.mult).then_inc(ap_n[n].sem, 1)

            def norm0(g, b):
                dve.wait_ge(emptied[XB.of(("project", b))], XB.through(("project", b), g))
                statistics(g, b, 0, xin, EPS0)

            def apply0(g, b):
                apply_norm(g, b, 0, xin, xin)

            def norm1(g, b):
                dve.wait_ge(betad.sem, betad.after(g, b + 1))
                statistics(g, b, 1, xin, EPS)

            def apply1(g, b):
                apply_norm(g, b, 1, xin, lnb)
                if b == NB - 1:
                    dve.wait_ge(rows_saved.sem, rows_saved.after(g, 1))
                    nc.vector.tensor_copy(xnT[:, :, :, 0], prev[:, :, :, 1]).then_inc(rows_copied.sem, 1)

            def shift(g, _):
                dve.wait_ge(emptied[XB.of(("turn_n", 1))], XB.through(("turn_n", 1), g))
                dve.wait_ge(rows_copied.sem, rows_copied.after(g, 1))
                tt(sx[:], xnT[:, :, :, 0:L], xnT[:, :, :, 1:], ALU.subtract).then_inc(shifted.sem, 1)
                dve.wait_ge(shifted.sem, shifted.after(g, 1))
                for c in range(NC):
                    stt(out=x5[:, 0, c], in0=sx[:, c], scalar=col("maa_x", c), in1=xnT[:, c, :, 1:],
                        op0=ALU.mult, op1=ALU.add).then_inc(mixed0.sem, 1)

            def mix(g, k):
                f = MIX[k]
                if k == 0:
                    dve.wait_ge(filled[XB.of(("low", 0))], XB.through(("low", 0), g))
                elif k == 2:
                    dve.wait_ge(filled[XB.of(("tdecay", 0))], XB.through(("tdecay", 0), g))
                elif k >= 3:
                    dve.wait_ge(filled[XB.of(("proj", 2 * k - 3))], XB.through(("proj", 2 * k - 3), g))
                for p in range(2):
                    bi = XB.of(("mix", 2 * k + p))
                    ps = bank[bi]
                    dve.wait_ge(filled[bi], XB.through(("mix", 2 * k + p), g))
                    for q in range(2):
                        c = 2 * p + q
                        last = stt(out=x5[:, k % 2, c], in0=ps[:, q * T:(q + 1) * T].rearrange(
                            "p (b t) -> p b t", b=NB), scalar=col("maa", f * NC + c), in1=sx[:, c],
                            op0=ALU.add, op1=ALU.mult)
                    last.then_inc(emptied[bi], 1)

            def keep_row(g, _):
                dve.wait_ge(rows_saved.sem, rows_saved.after(g, 1))
                nc.vector.tensor_copy(prev2[:], prev[:, :, :, 0]).then_inc(row_kept.sem, 1)

            def proj(g, k):
                if k == 3:
                    for p in range(2):
                        bi = XB.of(("proj", 2 * k + p))
                        ps = bank[bi]
                        dve.wait_ge(filled[bi], XB.through(("proj", 2 * k + p), g))
                        dve.wait_ge(v_rounded.sem, v_rounded.after(g, p + 1))
                        pair = slice(2 * p, 2 * p + 2)
                        tt(v_lo[:, pair, :], ps[:].rearrange("p (c n) -> p c n", c=2),
                           v_hi[:, pair, :].bitcast(F32), ALU.subtract).then_inc(emptied[bi], 1)
                if k < 4:
                    return
                for p in range(2):
                    bi = XB.of(("proj", 2 * k + p))
                    ps = bank[bi]
                    dve.wait_ge(filled[bi], XB.through(("proj", 2 * k + p), g))
                    dve.wait_ge(gate_th.sem, gate_th.after(g, p + 1))
                    stt(out=gT[:, 2 * p:2 * p + 2, :], in0=gth[:, 2 * p:2 * p + 2].rearrange(
                        "p c b t -> p c (b t)"), scalar=1.0, in1=ps[:].rearrange("p (c n) -> p c n", c=2),
                        op0=ALU.add, op1=ALU.mult).then_inc(emptied[bi], 1)

            def mean(g, p):
                dve.wait_ge(emptied[YB.of(("readout", 2 * p + 1))], YB.through(("readout", 2 * p + 1), g))
                bi = YB.of(("mean", p))
                ps = bank[bi]
                dve.wait_ge(filled[bi], YB.through(("mean", p), g))
                v = att[:, 2 * p:2 * p + 2, :]
                tt(v, v, ps[:].rearrange("p (c n) -> p c n", c=2), ALU.subtract).then_inc(emptied[bi], 1)

            def var(g, _):
                y, h = dg[:, 0, :], dg[:, 1, :]
                bi = YB.of(("var", 0))
                ps = bank[bi]
                dve.wait_ge(filled[bi], YB.through(("var", 0), g))
                ts(vs[:], ps[:, 0:T], EPS, None, ALU.add).then_inc(emptied[bi], 1)
                dve.wait_ge(emptied[bi], YB.through(("var", 0), g))
                ts(h.bitcast(I32), vs[:].bitcast(I32), 1, None, ALU.logical_shift_right).then_inc(newton.sem, 1)
                dve.wait_ge(newton.sem, newton.after(g, 1))
                ts(y.bitcast(I32), h.bitcast(I32), -1.0, float(0x5F3759DF), ALU.mult, ALU.add).then_inc(newton.sem, 1)
                for n in range(3):
                    dve.wait_ge(newton.sem, newton.after(g, 3 * n + 2))
                    tt(h, y, y, ALU.mult).then_inc(newton.sem, 1)
                    dve.wait_ge(newton.sem, newton.after(g, 3 * n + 3))
                    stt(out=h, in0=h, scalar=-0.5, in1=vs[:], op0=ALU.mult, op1=ALU.mult).then_inc(newton.sem, 1)
                    dve.wait_ge(newton.sem, newton.after(g, 3 * n + 4))
                    stt(out=y, in0=h, scalar=1.5, in1=y, op0=ALU.add, op1=ALU.mult).then_inc(newton.sem, 1)

            def groupnorm(g, _):
                pair = [slice(0, 2), slice(2, 4)]
                for p in range(2):
                    bi = YB.of(("spread", p))
                    ps = bank[bi]
                    dve.wait_ge(filled[bi], YB.through(("spread", p), g))
                    tt(att[:, pair[p], :], att[:, pair[p], :], ps[:].rearrange("p (c n) -> p c n", c=2),
                       ALU.mult).then_inc(emptied[bi], 1)
                for p in range(2):
                    dve.wait_ge(emptied[YB.of(("spread", p))], YB.through(("spread", p), g))
                    for c in (2 * p, 2 * p + 1):
                        last = ts(att[:, c, :], att[:, c, :], col("gn_w", c), col("gn_b", c), ALU.mult, ALU.add)
                    last.then_inc(gn_af.sem, 1)
                for p in range(2):
                    dve.wait_ge(gn_af.sem, gn_af.after(g, p + 1))
                    dve.wait_ge(emptied[XB.of(("proj", 8 + p))], XB.through(("proj", 8 + p), g))
                    stt(out=att[:, pair[p], :], in0=gT[:, pair[p], :], scalar=0.5, in1=att[:, pair[p], :],
                        op0=ALU.mult, op1=ALU.mult).then_inc(gated.sem, 1)

            def out_(g, b):
                if b == 0:
                    dve.wait_ge(kept.sem, kept.after(g, NB))
                bi = YB.of(("out", b))
                ps = bank[bi]
                dve.wait_ge(filled[bi], YB.through(("out", b), g))
                tt(keep[:, b, :], ps[:], keep[:, b, :], ALU.add).then_inc(emptied[bi], 1)

            def norm2(g, b):
                dve.wait_ge(emptied[YB.of(("out", b))], YB.through(("out", b), g))
                statistics(g, b, 2, keep, EPS)

            def apply2(g, b):
                if b == 0:
                    dve.wait_ge(squared.sem, squared.after(g, 2))
                apply_norm(g, b, 2, keep, ln2)
                if b == NB - 1:
                    dve.wait_ge(row_kept.sem, row_kept.after(g, 1))
                    nc.vector.tensor_copy(mnT[:, :, :, 0], prev2[:]).then_inc(rows2.sem, 1)

            def shift2(g, _):
                dve.wait_ge(emptied[YB.of(("turn_m", 1))], YB.through(("turn_m", 1), g))
                dve.wait_ge(rows2.sem, rows2.after(g, 1))
                tt(sx2[:], mnT[:, :, :, 0:L], mnT[:, :, :, 1:], ALU.subtract).then_inc(shifted2.sem, 1)
                dve.wait_ge(shifted2.sem, shifted2.after(g, 1))
                for dst, name, sig in ((xk, "mk", mixk), (xr, "mr", mixr)):
                    for c in range(NC):
                        stt(out=dst[:, c], in0=sx2[:, c], scalar=col(name, c), in1=mnT[:, c, :, 1:],
                            op0=ALU.mult, op1=ALU.add).then_inc(sig.sem, 1)

            def ffn_v(g, b):
                dve.wait_ge(emptied[YB.of(("ffn_r", b))], YB.through(("ffn_r", b), g))
                bi = YB.of(("ffn_v", b))
                ps = bank[bi]
                dve.wait_ge(filled[bi], YB.through(("ffn_v", b), g))
                stt(out=rr[:, b, :], in0=rr[:, b, :], scalar=1.0, in1=ps[:], op0=ALU.add,
                    op1=ALU.mult).then_inc(emptied[bi], 1)
                dve.wait_ge(emptied[YB.of(("ffn_v", b))], YB.through(("ffn_v", b), g))
                stt(out=keep[:, b, :], in0=rr[:, b, :], scalar=0.5, in1=keep[:, b, :], op0=ALU.mult,
                    op1=ALU.add).then_inc(final.sem, 1)

            BD = dict(norm0=norm0, apply0=apply0, norm1=norm1, apply1=apply1, norm2=norm2, apply2=apply2, shift=shift, mix=mix, keep=keep_row, proj=proj, mean=mean, var=var, groupnorm=groupnorm,
                      out=out_, shift2=shift2, ffn_v=ffn_v, unit=unit)

            def db(gd, gb):
                for sec, name, n in DB_STEPS:
                    g = gd if sec == "D" else gb
                    if g is not None and name in BD:
                        BD[name](g, n)

            sections(dve, ca, db)


def kernel(**inputs):
    import numpy as np
    import concourse.bacc as bacc
    from concourse.bass_utils import run_bass_kernel_spmd

    a = {n: np.asarray(v) for n, v in inputs.items()}
    L0 = {n[9:]: v for n, v in a.items() if n.startswith("L0_xattn_")}
    L1 = {n[9:]: v for n, v in a.items() if n.startswith("L1_xattn_")}

    def by_chunk(v):
        return v.reshape(-1, P).T

    def values_first(m):
        s = m.shape[:-1]
        return np.swapaxes(m.reshape(*s, NC, HC, HD), -1, -2).reshape(*s, E)

    def query_order(m):
        s = m.shape[:-1]
        return np.swapaxes(m.reshape(*s, KVH, GRP, HD), -3, -2).reshape(*s, E)

    columns = np.concatenate([
        by_chunk(query_order(L0["bq"])), by_chunk(L0["bk"]), by_chunk(L1["ln1_w"]), by_chunk(L1["ln1_b"]),
        by_chunk(L1["ln2_w"]), by_chunk(L1["ln2_b"]), by_chunk(L1["maa_x"]),
        *[by_chunk(L1["maa_stack"][f]) for f in range(5)], by_chunk(L1["time_decay"]),
        by_chunk(L1["faaaa"].reshape(E)), by_chunk(values_first(L1["gn_w"])), by_chunk(values_first(L1["gn_b"])),
        by_chunk(L1["ffn_maa_k"]), by_chunk(L1["ffn_maa_r"])], axis=1)
    rows = np.concatenate([L0["bo"], L0["gamma"], L0["beta"], L0["bv"]])[None]

    f = np.float32
    p = np.arange(P)
    ident = np.eye(P, dtype=f)
    meanb = (p[:, None] % HC == p[None] % HC).astype(f) / f(HD)
    headb = (p[:, None] // HD == p[None] % HC).astype(f)
    parity = (p[:, None] // HD % 2 == np.arange(2)[None]).astype(f)
    ebase = (p[:, None] // HD == np.arange(56)[None] - 24).astype(f)
    consts = np.concatenate([ident, meanb, headb, parity, ebase], axis=1)
    sel = (p[:, None, None] == np.arange(HD)[None, :, None] * HC + p[None, None] // HD).astype(f)

    bsel = (p[:, None, None] == 32 * np.arange(NC)[None, :, None] + p[None, None] % HC).astype(f)

    host = {
        "x": a["x"], "ctx": a["ctx_2048"], "mask": a["mask_Bx1xSxS2_ff0"],
        "consts": consts, "columns": columns, "rows": rows, "sel": sel, "bsel": bsel,
        "wq": query_order(L0["Wq"]), "wk": L0["Wk"], "wv": L0["Wv"], "wo": query_order(L0["Wo"].T).T,
        "w1": L1["maa_w1"], "w2": L1["maa_w2"].reshape(5 * MAA, E), "dw1": L1["decay_w1"], "dw2": L1["decay_w2"],
        "wr": L1["Wr"].T, "wkk": L1["Wk"].T, "wvv": values_first(L1["Wv"].T), "wg": values_first(L1["Wg"].T),
        "wo2": values_first(L1["Wo"]).T, "fk": L1["ffn_Wk"].T, "fr": L1["ffn_Wr"].T, "fv": L1["ffn_Wv"].T,
    }
    nc = bacc.Bacc("TRN2", target_bir_lowering=False, num_devices=1, dynamic_dma_scratch_size=1024)
    arrays, ap = {}, {}
    for name, v in host.items():
        v = np.ascontiguousarray(v)
        arrays[f"in_{name}"] = v
        ap[name] = nc.dram_tensor(f"in_{name}", v.shape, mybir.dt.from_np(v.dtype), kind="ExternalInput").ap()
    out = nc.dram_tensor("out", (B, L, E), F32, kind="ExternalOutput").ap()
    weights = {n: ap[n] for n in host if n not in ("x", "ctx", "mask")}
    build(nc, ap["x"], ap["ctx"], ap["mask"], weights, out)
    r = run_bass_kernel_spmd(nc, [arrays], core_ids=[0])
    return r.results[0]["out"]
```
